# Optimizing a Trainium2 kernel written in Bass

```python
import numpy as np
import jax
import jax.numpy as jnp

def _softmax(x, axis=-1):
    return jax.nn.softmax(x, axis=axis)

def _gelu(x):
    return jax.nn.gelu(x, approximate=True)

def _silu(x):
    return jax.nn.silu(x)

def _sigmoid(x):
    return jax.nn.sigmoid(x)

def _layernorm(x, axis=-1, eps=1e-05):
    m = jnp.mean(x, axis=axis, keepdims=True)
    v = jnp.var(x, axis=axis, keepdims=True)
    return (x - m) / jnp.sqrt(v + eps)

def _scatter_add(tgt, idx, src, axis=0):
    return tgt.at[idx].add(src)

def _segment_sum(src, seg, n):
    return jax.ops.segment_sum(src, seg, n)
kernel_name = 'mk_gnn_resnorm_d2_gnn_r8_371765'

def setup_inputs(seed: int=0):
    np.random.seed(seed)
    _w = jnp.asarray

    def _rec_inputs():
        import jax
        import jax.numpy as jnp
        _gk = jax.random.key(seed)
        x = -0.0006008 + 1.001 * jax.random.normal(jax.random.fold_in(_gk, 1), (6250, 256), jnp.float32)
        _s = jax.random.randint(jax.random.fold_in(_gk, 2), (50000,), 0, 6250, jnp.int32)
        _d = jax.random.randint(jax.random.fold_in(_gk, 3), (50000,), 0, 6250, jnp.int32)
        _loop = jnp.arange(6250, dtype=jnp.int32)
        src = jnp.concatenate([_s, _d, _loop])
        dst = jnp.concatenate([_d, _s, _loop])
        _o = jnp.argsort(dst, stable=True)
        src = src[_o]
        dst = dst[_o]
        edge_attr_64 = 0.000189758 + 1.00013 * jax.random.normal(jax.random.fold_in(_gk, 11), (106250, 64), jnp.float32)
        return (x, src, dst, edge_attr_64)
    x, src, dst, edge_attr_64 = _rec_inputs()

    def _L0_gnn_setup():
        import jax, jax.numpy as jnp
        import numpy as np
        N_NODES = 1250
        key = jax.random.key(seed)
        k1, k2, k3, k4 = jax.random.split(key, 4)
        h = jax.random.normal(k1, (N_NODES, 256), dtype=jnp.float32)
        edge_index = jax.random.randint(k2, (2, 40000), 0, N_NODES, dtype=jnp.int64)
        W = jax.random.normal(k3, (256, 512), dtype=jnp.float32) * (1.0 / np.sqrt(512.0))
        b = jax.random.normal(k4, (256,), dtype=jnp.float32) * 0.01
        return {'h': h, 'edge_index': edge_index, 'W': W, 'b': b}
    _L0_gnn_all = _L0_gnn_setup()
    _L0_gnn_in = {k: v for k, v in _L0_gnn_all.items() if k in ('W', 'b')}
    del _L0_gnn_all

    def _L1_gnn_setup():
        import jax, jax.numpy as jnp
        import numpy as np
        N, E = (6250, 100000)
        HID, EDIM, HEADS = (256, 64, 8)
        C = HID // HEADS
        NEG_SLOPE = 0.2
        LN_EPS = 1e-05

        def _gat_block(x, edge_index, edge_attr, W, W_e, att_src, att_dst, att_edge, bias, gamma, beta):
            n = x.shape[0]
            src, dst = (edge_index[0], edge_index[1])
            xp = (x @ W).reshape(n, HEADS, C)
            a_src = jnp.einsum('nhc,hc->nh', xp, att_src)
            a_dst = jnp.einsum('nhc,hc->nh', xp, att_dst)
            ep = (edge_attr @ W_e).reshape(-1, HEADS, C)
            a_edge = jnp.einsum('ehc,hc->eh', ep, att_edge)
            alpha = a_src[src] + a_dst[dst] + a_edge
            alpha = jax.nn.leaky_relu(alpha, NEG_SLOPE)
            m = jax.ops.segment_max(alpha, dst, num_segments=n)
            m = jnp.where(jnp.isfinite(m), m, 0.0)
            ea = jnp.exp(alpha - m[dst])
            den = jax.ops.segment_sum(ea, dst, num_segments=n)
            attn = ea / (den[dst] + 1e-16)
            msg = xp[src] * attn[:, :, None]
            out = jax.ops.segment_sum(msg, dst, num_segments=n)
            h = out.reshape(n, HEADS * C) + bias
            y = x + h
            mu = jnp.mean(y, axis=-1, keepdims=True)
            var = jnp.var(y, axis=-1, keepdims=True)
            return (y - mu) * jax.lax.rsqrt(var + LN_EPS) * gamma + beta
        key = jax.random.key(seed)
        ks = jax.random.split(key, 12)
        s = 1.0 / np.sqrt(HID)
        se = 1.0 / np.sqrt(EDIM)
        return {'x': jax.random.normal(ks[0], (N, HID), jnp.float32), 'edge_index': jax.random.randint(ks[1], (2, E), 0, N, jnp.int32), 'edge_attr': jax.random.normal(ks[2], (E, EDIM), jnp.float32), 'W': jax.random.uniform(ks[3], (HID, HEADS * C), jnp.float32, -s, s), 'W_e': jax.random.uniform(ks[4], (EDIM, HEADS * C), jnp.float32, -se, se), 'att_src': jax.random.normal(ks[5], (HEADS, C), jnp.float32) * 0.1, 'att_dst': jax.random.normal(ks[6], (HEADS, C), jnp.float32) * 0.1, 'att_edge': jax.random.normal(ks[7], (HEADS, C), jnp.float32) * 0.1, 'bias': jnp.zeros((HEADS * C,), jnp.float32), 'gamma': jnp.ones((HID,), jnp.float32), 'beta': jnp.zeros((HID,), jnp.float32)}
    _L1_gnn_all = _L1_gnn_setup()
    _L1_gnn_in = {k: v for k, v in _L1_gnn_all.items() if k in ('W', 'W_e', 'att_src', 'att_dst', 'att_edge', 'bias', 'gamma', 'beta')}
    del _L1_gnn_all
    return {'x': x, 'src': src, 'dst': dst, 'edge_attr_64': edge_attr_64, 'L0_gnn_W': _L0_gnn_in['W'], 'L0_gnn_b': _L0_gnn_in['b'], 'L1_gnn_W': _L1_gnn_in['W'], 'L1_gnn_W_e': _L1_gnn_in['W_e'], 'L1_gnn_att_src': _L1_gnn_in['att_src'], 'L1_gnn_att_dst': _L1_gnn_in['att_dst'], 'L1_gnn_att_edge': _L1_gnn_in['att_edge'], 'L1_gnn_bias': _L1_gnn_in['bias'], 'L1_gnn_gamma': _L1_gnn_in['gamma'], 'L1_gnn_beta': _L1_gnn_in['beta']}

def reference(x, src, dst, edge_attr_64, L0_gnn_W, L0_gnn_b, L1_gnn_W, L1_gnn_W_e, L1_gnn_att_src, L1_gnn_att_dst, L1_gnn_att_edge, L1_gnn_bias, L1_gnn_gamma, L1_gnn_beta):
    import jax
    import jax.numpy as jnp

    def _L0_gnn_ref(h, edge_index, W, b):
        import jax, jax.numpy as jnp
        import numpy as np
        N_NODES = 1250
        src, dst = (edge_index[0], edge_index[1])
        n = h.shape[0]
        msg_sum = jax.ops.segment_sum(h[src], dst, num_segments=n)
        deg = jax.ops.segment_sum(jnp.ones_like(src, dtype=h.dtype), dst, num_segments=n)
        agg = msg_sum / jnp.maximum(deg, 1.0)[:, None]
        h_total = jnp.concatenate([h, agg], axis=1)
        return h_total @ W.T + b

    def _L1_gnn_ref(x, edge_index, edge_attr, W, W_e, att_src, att_dst, att_edge, bias, gamma, beta):
        import jax, jax.numpy as jnp
        import numpy as np
        N, E = (6250, 100000)
        HID, EDIM, HEADS = (256, 64, 8)
        C = HID // HEADS
        NEG_SLOPE = 0.2
        LN_EPS = 1e-05

        def _gat_block(x, edge_index, edge_attr, W, W_e, att_src, att_dst, att_edge, bias, gamma, beta):
            n = x.shape[0]
            src, dst = (edge_index[0], edge_index[1])
            xp = (x @ W).reshape(n, HEADS, C)
            a_src = jnp.einsum('nhc,hc->nh', xp, att_src)
            a_dst = jnp.einsum('nhc,hc->nh', xp, att_dst)
            ep = (edge_attr @ W_e).reshape(-1, HEADS, C)
            a_edge = jnp.einsum('ehc,hc->eh', ep, att_edge)
            alpha = a_src[src] + a_dst[dst] + a_edge
            alpha = jax.nn.leaky_relu(alpha, NEG_SLOPE)
            m = jax.ops.segment_max(alpha, dst, num_segments=n)
            m = jnp.where(jnp.isfinite(m), m, 0.0)
            ea = jnp.exp(alpha - m[dst])
            den = jax.ops.segment_sum(ea, dst, num_segments=n)
            attn = ea / (den[dst] + 1e-16)
            msg = xp[src] * attn[:, :, None]
            out = jax.ops.segment_sum(msg, dst, num_segments=n)
            h = out.reshape(n, HEADS * C) + bias
            y = x + h
            mu = jnp.mean(y, axis=-1, keepdims=True)
            var = jnp.var(y, axis=-1, keepdims=True)
            return (y - mu) * jax.lax.rsqrt(var + LN_EPS) * gamma + beta
        return _gat_block(x, edge_index, edge_attr, W, W_e, att_src, att_dst, att_edge, bias, gamma, beta)
    edge_index = jnp.stack([src, dst])
    x = _layernorm(x + _L0_gnn_ref(x, edge_index, L0_gnn_W, L0_gnn_b), axis=-1)
    x = _layernorm(x + _L1_gnn_ref(x, edge_index, edge_attr_64, L1_gnn_W, L1_gnn_W_e, L1_gnn_att_src, L1_gnn_att_dst, L1_gnn_att_edge, L1_gnn_bias, L1_gnn_gamma, L1_gnn_beta), axis=-1)
    return x

_drawn_inputs = setup_inputs


def setup_inputs(seed=0):
    import zlib

    import numpy as np

    out = dict(_drawn_inputs(seed))
    spreads = {'L1_gnn_bias': (0.0, 0.1), 'L1_gnn_gamma': (1.0, 0.2), 'L1_gnn_beta': (0.0, 0.1)}
    factors = {'edge_attr_64': 3.047,
     'L0_gnn_b': 7.478,
     'L1_gnn_W_e': 2.982,
     'L1_gnn_att_dst': 57.216,
     'L1_gnn_att_edge': 2.922}
    for name, (base, spread) in spreads.items():
        noise = np.random.default_rng([zlib.crc32(name.encode()), seed]).standard_normal(out[name].shape)
        drawn = base * np.exp(spread * noise) if base else spread * noise
        out[name] = jnp.asarray(drawn.astype(out[name].dtype))
    for name, factor in factors.items():
        out[name] = (out[name] * factor).astype(out[name].dtype)
    return out
```

```python
import concourse.bass as bass
from concourse import mybir
from contextlib import ExitStack

P = 128
N, D, E, EDIM = 6250, 256, 106250, 64
HEADS = 8
C = D // HEADS
GROUP = 16
GROUPS = -(-E // (P * GROUP))
TILES = GROUP * GROUPS
BLOCKS = -(-N // P)
CHUNKS = 7
ROWS = CHUNKS * P
ACC = BLOCKS * P + P
XROW = D + HEADS
WIDE = XROW + HEADS
FULL, LEFT = E // P, E % P
BIG = 1.0e30
LN_EPS = 1.0e-5

fp32 = mybir.dt.float32
i32 = mybir.dt.int32
ALU = mybir.AluOpType
ACT = mybir.ActivationFunctionType
AX = mybir.AxisListType
ENGINE = mybir.EngineType


def wait(engine, semaphore, value):
    if isinstance(value, int) and value <= 0:
        return
    engine.wait_ge(semaphore, value)


class Order:

    def __init__(self, engine, semaphore, start):
        self.engine, self.semaphore, self.start, self.steps = engine, semaphore, start, 0

    def did(self, instruction):
        instruction.then_inc(self.semaphore, 1)
        self.steps += 1

    def settle(self):
        wait(self.engine, self.semaphore, self.start + self.steps)


def cols(start, size):
    return bass.ds(start, size) if not isinstance(start, int) else slice(start, start + size)


def tile_bases(nc, base_row, engine, first_tile):
    _, values = nc.values_load_multi_w_load_instructions(
        base_row[0:1, cols(first_tile, GROUP)], engines=(engine,), min_val=0, max_val=N,
        skip_runtime_bounds_check_because="they are node numbers, at most N for the padding")
    return values


def gnn_kernel(nc, x, src, dst, edge_attr, w0, b0, w1, w_e, att_src, att_dst, att_edge, bias, gamma, beta, out):
    ctx = ExitStack()
    with ctx:
        def sb(name, shape, dt=fp32):
            return ctx.enter_context(nc.sbuf_tensor(name, shape, dt))

        def sem(name):
            return ctx.enter_context(nc.semaphore(name))

        z_dram = nc.dram_tensor("z_dram", (BLOCKS * P, D), fp32).ap()
        x1_dram = nc.dram_tensor("x1_dram", (BLOCKS * P, D), fp32).ap()
        xp_dram = nc.dram_tensor("xp_dram", (BLOCKS * P, XROW), fp32).ap()
        adst_dram = nc.dram_tensor("adst_dram", (ACC, HEADS), fp32).ap()
        cut_dram = nc.dram_tensor("cut_dram", (ROWS * P,), fp32)

        PS = [ctx.enter_context(nc.psum_tensor(f"bank{i}", [P, 512], fp32)) for i in range(8)]

        acc = sb("acc", [P, 3, ACC])
        srcT = sb("srcT", [P, ROWS], i32)
        relT = sb("relT", [P, ROWS])
        base_row = sb("base_row", [1, ROWS], i32)
        a_edge = sb("a_edge", [P, TILES * HEADS])
        ident = sb("ident", [P, P])
        iota = sb("iota", [P, P])
        head_of = sb("head_of", [P, HEADS])
        tile_of = sb("tile_of", [P, GROUP])
        head_row = sb("head_row", [HEADS, P])
        spread = sb("spread", [P, 3, P])

        region = sb("region", [P, 4 * GROUP * XROW])
        taken = [0]

        def carve(*shape):
            size = 1
            for n in shape:
                size *= n
            v = region[:, taken[0]:taken[0] + size]
            taken[0] += size
            if len(shape) == 2:
                v = v.rearrange("p (a b) -> p a b", a=shape[0])
            if len(shape) == 3:
                v = v.rearrange("p (a b c) -> p a b c", a=shape[0], b=shape[1])
            return v

        w_self = carve(2, D)
        w_agg = carve(2, D)
        w_wide = carve(2, WIDE)
        b0_all = carve(D)
        v_edge = carve(2 * HEADS)
        ones = carve(P)
        rdeg = carve(BLOCKS)
        contB = carve(ROWS)
        shared = taken[0]

        dcur = carve(CHUNKS, P)
        dprev = carve(CHUNKS, P)
        srcf = carve(CHUNKS, P)
        diff = carve(CHUNKS, P)
        cut = carve(CHUNKS, P)
        rel = carve(CHUNKS, P)
        cont = carve(CHUNKS)
        w0_in = carve(2, 2 * D)
        w1_in = carve(2, D)
        we_in = carve(D)
        att_b = carve(3, D)
        prod = carve(3, D)
        d_i = sb("d_i", [P, 3, CHUNKS * P], i32) if False else None
        ints = region[:, taken[0]:taken[0] + 3 * ROWS].bitcast(i32).rearrange("p (a c e) -> p a c e", a=3, c=CHUNKS)
        taken[0] += 3 * ROWS
        assert taken[0] <= 4 * GROUP * XROW, taken[0]

        with ExitStack() as phase:
            blank = phase.enter_context(nc.semaphore("index_blank"))
            loaded = phase.enter_context(nc.semaphore("index_loaded"))
            weights = phase.enter_context(nc.semaphore("weights_loaded"))
            made = phase.enter_context(nc.semaphore("constants_made"))
            cast = phase.enter_context(nc.semaphore("vector_steps"))
            turned = phase.enter_context(nc.semaphore("indices_turned"))
            wturned = phase.enter_context(nc.semaphore("weights_turned"))
            stored = phase.enter_context(nc.semaphore("cuts_stored"))
            maskt = phase.enter_context(nc.semaphore("masks_turned"))
            block = phase.enter_context(nc.Block())
            SRC, CUR, PREV = range(3)
            CASTS, WEIGHTS_READY = 6, 0

            @block.gpsimd
            def _(pool):
                nc.gpsimd.memset(ints[:, SRC, :, :], 0)
                nc.gpsimd.memset(ints[:, CUR, :, :], N)
                nc.gpsimd.memset(ints[:, PREV, :, :], N).then_inc(blank, 1)
                pool.wait_ge(blank, 1)
                nc.gpsimd.memset(ints[0:1, PREV, 0, 0:1], -1).then_inc(blank, 1)
                nc.gpsimd.memset(ones, 1.0)
                nc.gpsimd.memset(v_edge, 0.0)
                nc.gpsimd.iota(iota[:, :], [[1, P]], base=0, channel_multiplier=0,
                               allow_small_or_imprecise_dtypes=True)
                nc.gpsimd.memset(ident[:, :], 0.0).then_inc(made, 1)
                pool.wait_ge(made, 1)
                nc.gpsimd.affine_select(out=ident[:, :], in_=ident[:, :], compare_op=ALU.not_equal, fill=1.0,
                                        base=0, pattern=[[-1, P]], channel_multiplier=1).then_inc(made, 1)
                nc.gpsimd.memset(acc[:, :, :], 0.0).then_inc(made, 1)

            @block.sync
            def _(sp):
                sp.wait_ge(blank, 2)
                whole = 6 * P * P
                rest = FULL - 6 * P

                def rows(first, n):
                    return n * P

                for which, array in ((SRC, src), (CUR, dst)):
                    sp.dma_start(ints[:, which, 0:6, :], array[0:whole].rearrange("(c t e) -> t c e", c=6, e=P)).then_inc(loaded, 16)
                    sp.dma_start(ints[0:rest, which, 6, :], array[whole:FULL * P].rearrange("(t e) -> t e", e=P)).then_inc(loaded, 16)
                    sp.dma_start(ints[rest:rest + 1, which, 6, 0:LEFT], array[FULL * P:E].rearrange("(t e) -> t e", t=1)).then_inc(loaded, 16)
                sp.dma_start(ints[0:1, PREV, 0, 1:P], dst[0:P - 1].rearrange("(t e) -> t e", t=1)).then_inc(loaded, 16)
                sp.dma_start(ints[1:P, PREV, 0, :], dst[P - 1:P - 1 + (P - 1) * P].rearrange("(t e) -> t e", e=P)).then_inc(loaded, 16)
                sp.dma_start(ints[:, PREV, 1:6, :], dst[P * P - 1:whole - 1].rearrange("(c t e) -> t c e", c=5, e=P)).then_inc(loaded, 16)
                sp.dma_start(ints[0:rest, PREV, 6, :], dst[whole - 1:FULL * P - 1].rearrange("(t e) -> t e", e=P)).then_inc(loaded, 16)
                sp.dma_start(ints[rest:rest + 1, PREV, 6, 0:LEFT + 1], dst[FULL * P - 1:E].rearrange("(t e) -> t e", t=1)).then_inc(loaded, 16)
                sp.wait_ge(cast, CASTS)
                sp.dma_start(cut_dram.ap().rearrange("(c t e) -> t c e", c=CHUNKS, e=P), cut).then_inc(stored, 16)
                sp.wait_ge(stored, 16)

            @block.scalar
            def _(act):
                act.dma_start(w0_in, w0.rearrange("(k p) i -> p k i", p=P)).then_inc(weights, 16)
                act.dma_start(w1_in, w1.rearrange("(k p) o -> p k o", p=P)).then_inc(weights, 16)
                act.dma_start(we_in[0:EDIM, :], w_e[:, :]).then_inc(weights, 16)
                act.dma_start(we_in[EDIM:2 * EDIM, :], w_e[:, :]).then_inc(weights, 16)
                for n, att in enumerate((att_src, att_dst, att_edge)):
                    act.dma_start(att_b[:, n, :], att.rearrange("h c -> (h c)").partition_broadcast(P)).then_inc(weights, 16)
                act.dma_start(b0_all, b0.partition_broadcast(P)).then_inc(weights, 16)
                act.wait_ge(turned, 1)
                for n in range(2):
                    width = 4 * P if n == 0 else 3 * P
                    nc.scalar.copy(relT[:, 4 * P * n:4 * P * n + width], PS[n][:, 0:width])
                    nc.scalar.copy(srcT[:, 4 * P * n:4 * P * n + width], PS[2 + n][:, 0:width])
                    nc.scalar.copy(contB[:, 4 * P * n:4 * P * n + width], PS[4 + n][:, 0:width])
                    nc.scalar.copy(base_row[0:1, 4 * P * n:4 * P * n + width], PS[6 + n][0:1, 0:width])
                act.drain().then_inc(maskt, 1)
                act.wait_ge(wturned, 1)
                nc.scalar.copy(w_self[:, :, :].rearrange("p a b -> p (a b)"), PS[0][:, :])
                nc.scalar.copy(w_agg[:, :, :].rearrange("p a b -> p (a b)"), PS[1][:, :])
                nc.scalar.copy(head_row[:, :], PS[2][0:HEADS, 0:P])

            @block.vector
            def _(dve):
                order = Order(dve, cast, 0)
                dve.wait_ge(loaded, 16 * 11)
                order.did(nc.vector.tensor_copy(srcf, ints[:, SRC, :, :]))
                order.did(nc.vector.tensor_copy(dcur, ints[:, CUR, :, :]))
                order.did(nc.vector.tensor_copy(dprev, ints[:, PREV, :, :]))
                order.settle()
                order.did(nc.vector.tensor_tensor(rel, dcur, dcur[:, :, 0:1].to_broadcast([P, CHUNKS, P]), ALU.subtract))
                order.did(nc.vector.tensor_tensor(diff, dcur, dprev, ALU.subtract))
                order.settle()
                order.did(nc.vector.tensor_scalar(cut, diff, -BIG, None, ALU.mult))
                assert order.steps == CASTS
                order.did(nc.vector.tensor_scalar(cont, diff[:, :, 0], -1.0, 1.0, ALU.mult, ALU.add))
                dve.wait_ge(made, 2)
                th = ident[:, :].rearrange("p (t h) -> p t h", h=HEADS)
                order.did(nc.vector.tensor_reduce(head_of[:, :], th.rearrange("p t h -> p h t"), AX.X, ALU.add))
                order.did(nc.vector.tensor_reduce(tile_of[:, :], th, AX.X, ALU.add))
                order.settle()
                for k in range(2):
                    order.did(nc.vector.tensor_copy(spread[:, k, :].rearrange("p (h c) -> p h c", c=C),
                                                    head_of[:, 4 * k:4 * k + 4].unsqueeze(2).to_broadcast([P, 4, C])))
                order.did(nc.vector.tensor_copy(spread[:, 2, 0:HEADS], head_of[:, :]))
                order.did(nc.vector.memset(spread[:, 2, HEADS:P], 0.0))
                dve.wait_ge(weights, 16 * 8)
                for n in range(2):
                    order.did(nc.vector.tensor_copy(w_wide[:, :, 0:D], w1_in) if n == 0 else
                              nc.vector.tensor_tensor(prod[:, 2, :], we_in, att_b[:, 2, :], ALU.mult))
                for n in range(2):
                    for k in range(2):
                        order.settle()
                        order.did(nc.vector.tensor_tensor(prod[:, k, :], w1_in[:, k, :], att_b[:, n, :], ALU.mult))
                        order.settle()
                        order.did(nc.vector.tensor_reduce(w_wide[:, k, D + HEADS * n:D + HEADS * (n + 1)],
                                                          prod[:, k, :].rearrange("p (h c) -> p h c", c=C), AX.X, ALU.add))
                for n in range(2):
                    half = slice(EDIM * n, EDIM * (n + 1))
                    order.did(nc.vector.tensor_reduce(v_edge[half, HEADS * n:HEADS * (n + 1)],
                                                      prod[half, 2, :].rearrange("p (h c) -> p h c", c=C), AX.X, ALU.add))
                order.settle()

            @block.tensor
            def _(pe):
                pe.wait_ge(made, 2)
                pe.wait_ge(cast, CASTS + 1)
                for c in range(CHUNKS):
                    at = slice(P * (c % 4), P * (c % 4) + P)
                    nc.tensor.transpose(PS[c // 4][:, at], rel[:, c, :], ident[:, :])
                    nc.tensor.transpose(PS[2 + c // 4][:, at], srcf[:, c, :], ident[:, :])
                    nc.tensor.matmul(PS[4 + c // 4][:, at], cont[:, c:c + 1].to_broadcast([P, P]), ident[:, :], start=True, stop=True)
                    last = nc.tensor.transpose(PS[6 + c // 4][0:1, at], dcur[:, c, 0:1], ident[:, :])
                last.then_inc(turned, 1)
                pe.wait_ge(maskt, 1)
                pe.wait_ge(weights, 16 * 8)
                pe.wait_ge(cast, CASTS + 3)
                for i in range(4):
                    for o in range(2):
                        nc.tensor.transpose(PS[i // 2][:, D * (i % 2) + P * o:D * (i % 2) + P * (o + 1)],
                                            w0_in[:, o, P * i:P * (i + 1)], ident[:, :])
                nc.tensor.transpose(PS[2][0:HEADS, 0:P], head_of[:, :], ident[:, :]).then_inc(wturned, 1)

        taken[0] = shared
        HALF = GROUP // 2
        ring = carve(2, GROUP, D)
        onehot = sb("onehot", [P, 2 * GROUP, P])
        edge_in = carve(2, GROUP * EDIM)
        edgeT = carve(2, 512)
        x_in = carve(2, D)
        xT = carve(2, D)
        z_out = carve(2, D)
        idx = sb("idx", [P, 4, GROUP], i32)
        assert taken[0] <= 4 * GROUP * XROW, taken[0]
        AGG = PS[0:4]
        TE, AE, ZB = PS[4:6], PS[6], PS[7]
        last_rows = N - (BLOCKS - 1) * P

        with ExitStack() as phase:
            def psem(name):
                return phase.enter_context(nc.semaphore(name))
            idx_ready = psem("idx0_ready")
            gathered = [[psem(f"gathered0_{p}{h}") for h in range(2)] for p in range(2)]
            gate = psem("gate0")
            onehot_ready = psem("onehot0_ready")
            agg_ready = psem("agg0_ready")
            acc_copied = psem("acc0_copied")
            agg_free = psem("agg0_free")
            edges_in = [psem(f"edges_in{p}") for p in range(2)]
            te_ready, te_copied = psem("te_ready"), psem("te_copied")
            ae_ready, ae_copied = psem("ae_ready"), psem("ae_copied")
            x_loaded = [psem(f"x_loaded{p}") for p in range(2)]
            xt_ready, xt_copied = psem("xt_ready"), psem("xt_copied")
            z_ready, z_summed = psem("z_ready"), psem("z_summed")
            z_stored = [psem(f"z_stored{p}") for p in range(2)]
            zeros_out = psem("adst_zeroed")
            xblank = psem("x_blank")
            zsum = psem("z_sum_steps")
            block = phase.enter_context(nc.Block())

            def pairs(engine, body):
                for u in range(2):
                    body(u, u, 0)
                with engine.Fori(1, 24) as i:
                    for u in range(2):
                        body(2 * i + u, u, i)
                for s in range(48, GROUPS):
                    body(s, s % 2, s // 2)

            def has_block(s):
                return not isinstance(s, int) or s < BLOCKS

            @block.gpsimd
            def _(pool):
                def group(s, u, i):
                    wait(pool, idx_ready, s + 1)
                    for h in range(2):
                        wait(pool, agg_ready, GROUP * (s - 2) + HALF * (h + 1))
                        pool.sem_inc(gate, 1)
                        for t in range(HALF * h, HALF * (h + 1)):
                            nc.gpsimd.indirect_dma_start(
                                out=ring[:, u, t, :], out_offset=None, in_=x[:, :],
                                in_offset=bass.IndirectOffsetOnAxis(ap=idx[:, u, t:t + 1], axis=0),
                            ).then_inc(gathered[u][h], 16)
                pairs(pool, group)

            @block.sync
            def _(sp):
                sp.wait_ge(xblank, 1)

                def load_edges(s, u):
                    if isinstance(s, int) and s == GROUPS - 1:
                        full = FULL - GROUP * s
                        sp.dma_start(edge_in[:, u, 0:full * EDIM].rearrange("p (t k) -> p t k", k=EDIM),
                                     edge_attr[GROUP * s * P:FULL * P, :].rearrange("(t p) k -> p t k", p=P)).then_inc(edges_in[u], 16)
                        sp.dma_start(edge_in[0:LEFT, u, full * EDIM:(full + 1) * EDIM],
                                     edge_attr[FULL * P:E, :]).then_inc(edges_in[u], 16)
                        return
                    sp.dma_start(edge_in[:, u, :].rearrange("p (t k) -> p t k", k=EDIM),
                                 edge_attr[cols(s * (GROUP * P), GROUP * P), :].rearrange("(t p) k -> p t k", p=P)).then_inc(edges_in[u], 16)

                def load_x(s, u):
                    n = last_rows if isinstance(s, int) and s == BLOCKS - 1 else P
                    sp.dma_start(x_in[0:n, u, :], x[cols(s * P, n), :]).then_inc(x_loaded[u], 16)

                def group(s, u, i):
                    if not isinstance(s, int) or s + 2 < GROUPS:
                        wait(sp, te_ready, 2 * s + 2)
                        load_edges(s + 2, u)
                    if has_block(s):
                        wait(sp, z_summed, s + 1)
                        sp.dma_start(z_dram[cols(s * P, P), :], z_out[:, u, :]).then_inc(z_stored[u], 16)
                    if not isinstance(s, int) or s + 2 < BLOCKS:
                        load_x(s + 2, u)

                for s in range(2):
                    load_edges(s, s)
                    load_x(s, s)

                sp.dma_start(adst_dram[BLOCKS * P:ACC, :], acc[:, 0, ACC - HEADS:ACC]).then_inc(zeros_out, 16)
                for u in range(2):
                    group(u, u, 0)
                with sp.Fori(1, 23) as i:
                    for u in range(2):
                        group(2 * i + u, u, i)
                for s in range(46, GROUPS):
                    group(s, s % 2, s // 2)
                sp.wait_ge(zeros_out, 16)
                sp.wait_ge(z_stored[0], 16 * 25)
                sp.wait_ge(z_stored[1], 16 * 24)

            @block.tensor
            def _(pe):
                def transposes(s, u, i, bank):
                    if bank == 0:
                        extra = 16 if isinstance(s, int) and s == GROUPS - 1 else 0
                        pe.wait_ge(edges_in[u], 16 * (i + 1) + extra)
                    wait(pe, te_copied, 2 * (s - 1) + bank + 1)
                    for j in range(4):
                        last = nc.tensor.transpose(TE[bank][:, P * j:P * (j + 1)],
                                                   edge_in[:, u, P * (4 * bank + j):P * (4 * bank + j + 1)], ident[:, :])
                    last.then_inc(te_ready, 1)

                def edge_products(s, u, bank):
                    pe.wait_ge(te_copied, 2 * s + bank + 1)
                    if bank == 0:
                        wait(pe, ae_copied, s)
                    for j in range(4):
                        q = 4 * bank + j
                        last = nc.tensor.matmul(AE[:, 16 * q:16 * (q + 1)], edgeT[:, bank, P * j:P * (j + 1)], v_edge,
                                                start=True, stop=True)
                    if bank == 1:
                        last.then_inc(ae_ready, 1)

                def group(s, u, i):
                    transposes(s, u, i, 0)
                    if has_block(s):
                        pe.wait_ge(x_loaded[u], 16 * (i + 1))
                        wait(pe, z_summed, s)
                        for k in range(2):
                            last = nc.tensor.transpose(ZB[:, P * k:P * (k + 1)], x_in[:, u, P * k:P * (k + 1)], ident[:, :])
                        last.then_inc(xt_ready, 1)
                    for t in range(GROUP):
                        if t == 3:
                            transposes(s, u, i, 1)
                        if t == 6:
                            edge_products(s, u, 0)
                        if t == 8 and has_block(s):
                            pe.wait_ge(xt_copied, s + 1)
                            for k in range(2):
                                last = nc.tensor.matmul(ZB[:, D:2 * D], xT[:, u, P * k:P * (k + 1)], w_self[:, k, :],
                                                        start=(k == 0), stop=(k == 1))
                            last.then_inc(z_ready, 1)
                        if t == 11:
                            edge_products(s, u, 1)
                        if t % HALF == 0:
                            pe.wait_ge(gathered[u][t // HALF], 16 * HALF * (i + 1))
                            pe.wait_ge(onehot_ready, 2 * s + t // HALF + 1)
                        wait(pe, agg_free, GROUP * s + t - 3)
                        hot = onehot[:, HALF * (t // HALF) + t % HALF, :]
                        bank = AGG[t % 4]
                        for k in range(2):
                            nc.tensor.matmul(bank[:, P * k:P * (k + 1)], ring[:, u, t, P * k:P * (k + 1)], hot, start=True, stop=True)
                        nc.tensor.matmul(bank[:, 2 * P:3 * P], ones[:, :], hot, start=True, stop=True).then_inc(agg_ready, 1)
                pairs(pe, group)

            @block.scalar
            def _(act):
                def group(s, u, i):
                    bases = tile_bases(nc, base_row, ENGINE.Activation, GROUP * s)
                    for t in range(GROUP):
                        if t == 1 and has_block(s):
                            act.wait_ge(xt_ready, s + 1)
                            wait(act, z_ready, s - 1)
                            nc.scalar.copy(xT[:, u, :], ZB[:, 0:D]).then_inc(xt_copied, 1)
                        act.wait_ge(agg_ready, GROUP * s + t + 1)
                        wait(act, acc_copied, GROUP * s + t)
                        act.sem_inc(gate, 1)
                        nc.scalar.copy(acc[:, :, bass.ds(bases[t] + 1, P - 1)],
                                       AGG[t % 4][:, 0:3 * P].rearrange("p (a b) -> p a b", a=3)[:, :, 1:P]).then_inc(acc_copied, 1)
                pairs(act, group)

            @block.vector
            def _(dve):
                def build_onehot(unit_tiles, rel_cols, h):
                    nc.vector.tensor_tensor(onehot[:, HALF * h:HALF * (h + 1), :],
                                            iota[:, :].unsqueeze(1).to_broadcast([P, HALF, P]),
                                            rel_cols.unsqueeze(2).to_broadcast([P, HALF, P]), ALU.is_equal).then_inc(onehot_ready, 1)

                def group(s, u, i):
                    bases = tile_bases(nc, base_row, ENGINE.DVE, GROUP * s)
                    for t in range(GROUP):
                        if t == 0 and (not isinstance(s, int) or s < GROUPS - 1):
                            pass
                        if t == 0:
                            wait(dve, agg_ready, GROUP * s)
                            build_onehot(None, relT[:, cols(GROUP * s + HALF, HALF)], 1)
                        if t == 2 and (not isinstance(s, int) or s + 2 < GROUPS):
                            dve.wait_ge(gathered[u][1], 16 * HALF * (i + 1))
                            nc.vector.tensor_copy(idx[:, u, :], srcT[:, cols(GROUP * s + 2 * GROUP, GROUP)]).then_inc(idx_ready, 1)
                        if t == 1 or t == 5:
                            bank = t // 4
                            dve.wait_ge(te_ready, 2 * s + bank + 1)
                            nc.vector.tensor_copy(edgeT[:, bank, :], TE[bank][:, :]).then_inc(te_copied, 1)
                        if t == 9 and (not isinstance(s, int) or s + 1 < GROUPS):
                            dve.wait_ge(agg_ready, GROUP * s + HALF)
                            build_onehot(None, relT[:, cols(GROUP * s + GROUP, HALF)], 0)
                        if t == 11 and has_block(s):
                            dve.wait_ge(z_ready, s + 1)
                            wait(dve, z_stored[u], 16 * i)
                            nc.vector.tensor_tensor(z_out[:, u, :], ZB[:, D:2 * D], x_in[:, u, :], ALU.add).then_inc(zsum, 1)
                            dve.wait_ge(zsum, s + 1)
                            nc.vector.tensor_tensor(z_out[:, u, :], z_out[:, u, :], b0_all, ALU.add).then_inc(z_summed, 1)
                        if t == 14:
                            dve.wait_ge(ae_ready, s + 1)
                            nc.vector.tensor_copy(a_edge[:, cols(P * s, P)], AE[:, 0:P]).then_inc(ae_copied, 1)
                        dve.wait_ge(acc_copied, GROUP * s + t + 1)
                        wait(dve, agg_free, GROUP * s + t)
                        col = acc[:, :, bass.ds(bases[t], 1)].rearrange("p a o -> p (a o)")
                        nc.vector.scalar_tensor_tensor(
                            out=col, in0=col, scalar=contB[:, cols(GROUP * s + t, 1)],
                            in1=AGG[t % 4][:, 0:3 * P].rearrange("p (a b) -> p a b", a=3)[:, :, 0],
                            op0=ALU.mult, op1=ALU.add).then_inc(agg_free, 1)

                nc.vector.memset(x_in[:, :, :], 0.0).then_inc(xblank, 1)
                for s in range(2):
                    nc.vector.tensor_copy(idx[:, s, :], srcT[:, GROUP * s:GROUP * (s + 1)]).then_inc(idx_ready, 1)
                build_onehot(None, relT[:, 0:HALF], 0)
                pairs(dve, group)
        taken[0] = shared
        z_in, staged, y_mid, x1_new, x1T = carve(2, D), carve(2, D), carve(2, D), carve(2, D), carve(2, D)
        x_wide = carve(2, WIDE)
        stats, moments, spreads = carve(2, 6), carve(2, 2), carve(2, 4)
        DEG = PS[6]

        def skewed(engine, body, depth):
            for j in range(4):
                body(j, j % 2, lambda lag, j=j: (j - lag) // 2)
            with engine.Fori(2, 24) as i:
                for u in range(2):
                    body(2 * i + u, u, lambda lag, u=u: i + (u - lag) // 2)
            for j in range(48, BLOCKS + depth):
                body(j, j % 2, lambda lag, j=j: (j - lag) // 2)

        def inside(b):
            return not isinstance(b, int) or 0 <= b < BLOCKS

        with ExitStack() as phase:
            def psem(name):
                return phase.enter_context(nc.semaphore(name))
            deg_ready, rdeg_steps = psem("degrees_ready"), psem("rdeg_steps")
            z_loaded = [psem(f"z_loaded{p}") for p in range(2)]
            staged_ready, self_ready = psem("staged_ready"), psem("product_ready")
            y_made, var_ready, sd_ready = psem("y_made"), psem("var_ready"), psem("sd_ready")
            x1_ready, x1t_ready, x1t_copied = psem("x1_ready"), psem("x1t_ready"), psem("x1t_copied")
            wide_ready, wide_copied = psem("wide_ready"), psem("wide_copied")
            x1_stored = [psem(f"x1_stored{p}") for p in range(2)]
            wide_stored = [psem(f"wide_stored{p}") for p in range(2)]
            stats_made, moments_made, rsd_made = psem("stats_made"), psem("moments_made"), psem("rsd_made")
            gate = psem("mid_gate")
            block = phase.enter_context(nc.Block())

            @block.sync
            def _(sp):
                def step(j, u, half):
                    if inside(j):
                        wait(sp, y_made, j - 1)
                        sp.dma_start(z_in[:, u, :], z_dram[cols(j * P, P), :]).then_inc(z_loaded[u], 16)
                    if inside(j - 1):
                        sp.wait_ge(x1_ready, j)
                        sp.dma_start(x1_dram[cols((j - 1) * P, P), :], x1_new[:, 1 - u, :]).then_inc(x1_stored[1 - u], 16)
                    if inside(j - 2):
                        sp.wait_ge(wide_copied, j - 1)
                        sp.dma_start(xp_dram[cols((j - 2) * P, P), :], x_wide[:, u, 0:XROW]).then_inc(wide_stored[u], 16)
                        sp.dma_start(adst_dram[cols((j - 2) * P, P), :], x_wide[:, u, XROW:WIDE]).then_inc(wide_stored[u], 16)
                skewed(sp, step, 2)
                for p in range(2):
                    sp.wait_ge(x1_stored[p], 16 * (25 - p))
                    sp.wait_ge(wide_stored[p], 32 * (25 - p))

            @block.tensor
            def _(pe):
                for b in range(BLOCKS):
                    last = nc.tensor.matmul(DEG[:, b:b + 1], acc[0:1, 2, P * b:P * (b + 1)], ones[0:1, 0:1], start=True, stop=True)
                last.then_inc(deg_ready, 1)

                def step(j, u, half):
                    if inside(j):
                        pe.wait_ge(staged_ready, j + 1)
                        wait(pe, y_made, j - 1)
                        for k in range(2):
                            last = nc.tensor.matmul(PS[u][:, 0:D], staged[:, u, P * k:P * (k + 1)], w_agg[:, k, :],
                                                    start=(k == 0), stop=(k == 1))
                        last.then_inc(self_ready, 1)
                    if inside(j - 1):
                        pe.wait_ge(x1_ready, j)
                        wait(pe, x1t_copied, j - 2)
                        for k in range(2):
                            last = nc.tensor.transpose(PS[3 - u][:, P * k:P * (k + 1)], x1_new[:, 1 - u, P * k:P * (k + 1)], ident[:, :])
                        last.then_inc(x1t_ready, 1)
                    if inside(j - 2):
                        pe.wait_ge(x1t_copied, j - 1)
                        wait(pe, wide_copied, j - 3)
                        for k in range(2):
                            last = nc.tensor.matmul(PS[4 + u][:, 0:WIDE], x1T[:, u, P * k:P * (k + 1)], w_wide[:, k, :],
                                                    start=(k == 0), stop=(k == 1))
                        last.then_inc(wide_ready, 1)
                skewed(pe, step, 2)

            @block.scalar
            def _(act):
                def step(j, u, half):
                    if inside(j):
                        wait(act, self_ready, j - 1)
                        act.sem_inc(gate, 1)
                        nc.scalar.copy(staged[:, u, :].rearrange("p (k n) -> p k n", k=2),
                                       acc[:, 0:2, cols(j * P, P)]).then_inc(staged_ready, 1)
                    if inside(j - 1):
                        act.wait_ge(x1t_ready, j)
                        wait(act, wide_ready, j - 2)
                        nc.scalar.copy(x1T[:, 1 - u, :], PS[3 - u][:, 0:D]).then_inc(x1t_copied, 1)
                    if inside(j):
                        act.wait_ge(var_ready, j + 1)
                        nc.scalar.activation(spreads[:, u, 1:2], spreads[:, u, 0:1], ACT.Sqrt).then_inc(sd_ready, 1)
                skewed(act, step, 2)

            @block.vector
            def _(dve):
                dve.wait_ge(deg_ready, 1)
                nc.vector.tensor_scalar(rdeg, DEG[:, 0:BLOCKS], 1.0, None, ALU.max).then_inc(rdeg_steps, 1)
                dve.wait_ge(rdeg_steps, 1)
                nc.vector.reciprocal(rdeg, rdeg).then_inc(rdeg_steps, 1)
                dve.wait_ge(rdeg_steps, 2)
                def step(j, u, half):
                    if inside(j - 1):
                        v = 1 - u
                        dve.wait_ge(sd_ready, j)
                        nc.vector.reciprocal(spreads[:, v, 2:3], spreads[:, v, 1:2]).then_inc(rsd_made, 1)
                        dve.wait_ge(rsd_made, j)
                        wait(dve, x1_stored[v], 16 * half(1))
                        nc.vector.tensor_scalar(x1_new[:, v, :], y_mid[:, v, :], moments[:, v, 0:1], spreads[:, v, 2:3],
                                                ALU.subtract, ALU.mult).then_inc(x1_ready, 1)
                    if inside(j):
                        dve.wait_ge(self_ready, j + 1)
                        dve.wait_ge(z_loaded[u], 16 * (half(0) + 1))
                        nc.vector.scalar_tensor_tensor(out=y_mid[:, u, :], in0=PS[u][:, 0:D], scalar=rdeg[:, cols(j, 1)],
                                                       in1=z_in[:, u, :], op0=ALU.mult, op1=ALU.add).then_inc(y_made, 1)
                        dve.wait_ge(y_made, j + 1)
                        nc.vector.bn_stats(stats[:, u, :], y_mid[:, u, :]).then_inc(stats_made, 1)
                        dve.wait_ge(stats_made, j + 1)
                        dve.sem_inc(gate, 1)
                        nc.vector.bn_aggr(moments[:, u, :], stats[:, u, :]).then_inc(moments_made, 1)
                        dve.wait_ge(moments_made, j + 1)
                        nc.vector.tensor_scalar(spreads[:, u, 0:1], moments[:, u, 1:2], LN_EPS, None, ALU.add).then_inc(var_ready, 1)
                    if inside(j - 2):
                        dve.wait_ge(wide_ready, j - 1)
                        wait(dve, wide_stored[u], 32 * half(2))
                        nc.vector.tensor_copy(x_wide[:, u, :], PS[4 + u][:, 0:WIDE]).then_inc(wide_copied, 1)
                skewed(dve, step, 2)

        SLOTS = 4
        rows = region[:, :].rearrange("p (s t f) -> p s t f", s=SLOTS, t=GROUP)
        hotT = sb("hotT", [P, 2, 4 * P])
        windows = sb("windows", [P, 2, GROUP, HEADS])
        cuts = sb("cuts", [P, 2, P + 1])
        logits = sb("logits", [P, P])
        scan_a = sb("scan_a", [P, P])
        scan_b = sb("scan_b", [P, P])
        below = sb("below", [P, P + 1])
        powers = sb("powers", [P, P + 1])
        weight = sb("weight", [P, 2, P + 3 * GROUP])
        ends = sb("ends", [P, 2 * GROUP])
        ends_cut = sb("ends_cut", [P, 1])
        ends_row = sb("ends_row", [HEADS, 2 * GROUP])
        running = sb("running", [HEADS, GROUP + 1])
        carried = sb("carried", [P, 1])
        picked = sb("picked", [P, GROUP])
        factors = sb("factors", [P, GROUP])
        AGG, TR, LOOK, VT, MS = PS[0:4], PS[4], PS[5], PS[6], PS[7]
        NSTEP = 13

        with ExitStack() as phase:
            def psem(name):
                return phase.enter_context(nc.semaphore(name))
            idx_ready = psem("idx1_ready")
            gathered = [psem(f"gathered1_{r}") for r in range(SLOTS)]
            gate = psem("gate1")
            fetched = [psem(f"windows_fetched{p}") for p in range(2)]
            hot_ready = psem("hot_ready")
            tr_ready, tr_copied = psem("tr_ready"), psem("tr_copied")
            looked_up = psem("looked_up")
            logits_ready, vt_ready = psem("logits_ready"), psem("vt_ready")
            ends_ready, ends_turned = psem("ends_ready"), psem("ends_turned")
            running_ready, carry_ready = psem("running_ready"), psem("carry_ready")
            below_ready, powers_ready = psem("below_ready"), psem("powers_ready")
            factors_ready, weight_turned, weight_ready = psem("factors_ready"), psem("weight_turned"), psem("weight_ready")
            weighted = psem("rows_weighted")
            agg_ready, acc_copied, agg_free = psem("agg1_ready"), psem("acc1_copied"), psem("agg1_free")
            scaled = psem("column_scaled")
            steps = psem("front_steps")
            block = phase.enter_context(nc.Block())

            def fours(engine, body):
                for s in range(4):
                    body(s, s, 0)
                with engine.Fori(1, 12) as i:
                    for u in range(4):
                        body(4 * i + u, u, i)
                for s in range(48, GROUPS):
                    body(s, s % 4, s // 4)

            def more(s, ahead=1):
                return not isinstance(s, int) or s + ahead < GROUPS

            def turn(s_index, u):
                return s_index + (u + 1) // 4 + 1

            @block.gpsimd
            def _(pool):
                def group(s, u, i):
                    pool.wait_ge(idx_ready, s + 1)
                    wait(pool, agg_ready, GROUP * (s - 3))
                    pool.sem_inc(gate, 1)
                    for t in range(GROUP):
                        nc.gpsimd.indirect_dma_start(
                            out=rows[:, u, t, :], out_offset=None, in_=xp_dram[:, :],
                            in_offset=bass.IndirectOffsetOnAxis(ap=idx[:, u, t:t + 1], axis=0),
                        ).then_inc(gathered[u], 16)
                fours(pool, group)

            @block.sync
            def _(sp):
                def fetch(q, p):
                    bases = tile_bases(nc, base_row, ENGINE.SP, GROUP * q)
                    wait(sp, below_ready, q - 1)
                    for t in range(GROUP):
                        sp.dma_start(windows[:, p, t, :], adst_dram[bass.ds(bases[t], P), :]).then_inc(fetched[p], 16)
                    sp.dma_start(cuts[:, p, :], bass.AP(tensor=cut_dram, offset=q * (GROUP * P),
                                                        ap=[[P, GROUP], [0, HEADS], [1, P + 1]])).then_inc(fetched[p], 16)

                def group(s, u, i):
                    if more(s):
                        fetch(s + 1, (u + 1) % 2)
                fetch(0, 0)
                fours(sp, group)

            FETCHES = 16 * (GROUP + 1)

            def fetches(s, u, i):
                if isinstance(s, int):
                    return FETCHES * ((s + 1) // 2 + 1)
                return FETCHES * (2 * i + (u + 1) // 2 + 1)

            @block.tensor
            def _(pe):
                def turn_onehot(q, p, g):
                    pe.wait_ge(hot_ready, 2 * q + g // 2 + 1)
                    wait(pe, tr_copied, 4 * q + g)
                    for j in range(4):
                        last = nc.tensor.transpose(TR[:, P * j:P * (j + 1)], onehot[:, GROUP * p + 4 * g + j, :], ident[:, :])
                    last.then_inc(tr_ready, 1)

                def look_up(q, p, g, fetch_count):
                    pe.wait_ge(tr_copied, 4 * q + g + 1)
                    if g == 0:
                        pe.wait_ge(fetched[p], fetch_count)
                        wait(pe, logits_ready, q)
                    for j in range(4):
                        t = 4 * g + j
                        last = nc.tensor.matmul(LOOK[:, HEADS * t:HEADS * (t + 1)], hotT[:, g % 2, P * j:P * (j + 1)],
                                                windows[:, p, t, :], start=True, stop=True)
                    last.then_inc(looked_up, 1)

                def front(q, p, k, fetch_count):
                    if k in (1, 3, 5, 7):
                        turn_onehot(q, p, k // 2)
                    if k in (3, 5, 7, 9):
                        look_up(q, p, (k - 3) // 2, fetch_count)
                    if k == 10:
                        pe.wait_ge(logits_ready, q + 1)
                        wait(pe, below_ready, q)
                        nc.tensor.transpose(VT[:, 0:P], logits[:, :], ident[:, :]).then_inc(vt_ready, 1)
                    if k == 11:
                        pe.wait_ge(ends_ready, q + 1)
                        nc.tensor.matmul(MS[0:HEADS, 0:2 * GROUP], head_of[:, :], ends[:, :], start=True, stop=True).then_inc(ends_turned, 1)
                    if k == 12:
                        pe.wait_ge(running_ready, q + 1)
                        nc.tensor.matmul(MS[:, 32:32 + GROUP], head_row[:, :], running[:, 0:GROUP], start=True, stop=True).then_inc(carry_ready, 1)
                    if k == 15:
                        pe.wait_ge(powers_ready, q + 1)
                        nc.tensor.transpose(MS[:, P:2 * P], powers[:, 0:P], ident[:, :])
                        pe.wait_ge(factors_ready, q + 1)
                        for n in range(3):
                            last = nc.tensor.matmul(MS[:, 2 * P + GROUP * n:2 * P + GROUP * (n + 1)], spread[:, n, :], factors[:, :],
                                                    start=True, stop=True)
                        last.then_inc(weight_turned, 1)

                def group(s, u, i):
                    p = u % 2
                    for t in range(GROUP):
                        if more(s):
                            front(s + 1, 1 - p, t, fetches(s, u, i))
                        if t % 4 == 0:
                            pe.wait_ge(weighted, 4 * s + t // 4 + 1)
                        wait(pe, agg_free, GROUP * s + t - 3)
                        bank = AGG[t % 4]
                        hot = onehot[:, GROUP * p + t, :]
                        for k in range(2):
                            nc.tensor.matmul(bank[:, P * k:P * (k + 1)], rows[:, u, t, P * k:P * (k + 1)], hot, start=True, stop=True)
                        nc.tensor.matmul(bank[0:HEADS, 2 * P:3 * P], weight[:, p, HEADS * t:HEADS * (t + 1)], hot, start=True, stop=True).then_inc(agg_ready, 1)

                for k in range(GROUP):
                    front(0, 0, k, FETCHES)
                fours(pe, group)

            @block.scalar
            def _(act):
                def front(q, k):
                    if k in (2, 4, 6, 8):
                        g = k // 2 - 1
                        act.wait_ge(tr_ready, 4 * q + g + 1)
                        wait(act, looked_up, 4 * q + g - 1)
                        nc.scalar.copy(hotT[:, g % 2, :], TR[:, :]).then_inc(tr_copied, 1)
                    if k == 14:
                        act.wait_ge(below_ready, q + 1)
                        nc.scalar.activation(powers[:, :], below[:, :], ACT.Exp).then_inc(powers_ready, 1)

                def group(s, u, i):
                    bases = tile_bases(nc, base_row, ENGINE.Activation, GROUP * s)
                    for t in range(GROUP):
                        if more(s):
                            front(s + 1, t)
                        act.wait_ge(agg_ready, GROUP * s + t + 1)
                        wait(act, acc_copied, GROUP * s + t)
                        act.sem_inc(gate, 1)
                        nc.scalar.copy(acc[:, :, bass.ds(bases[t] + 1, P - 1)],
                                       AGG[t % 4][:, 0:3 * P].rearrange("p (a b) -> p a b", a=3)[:, :, 1:P]).then_inc(acc_copied, 1)

                for k in range(GROUP):
                    front(0, k)
                fours(act, group)

            @block.vector
            def _(dve):
                def build(q, p, h):
                    nc.vector.tensor_tensor(onehot[:, GROUP * p + HALF * h:GROUP * p + HALF * (h + 1), :],
                                            iota[:, :].unsqueeze(1).to_broadcast([P, HALF, P]),
                                            relT[:, cols(GROUP * q + HALF * h, HALF)].unsqueeze(2).to_broadcast([P, HALF, P]),
                                            ALU.is_equal).then_inc(hot_ready, 1)

                def front(q, p, r, k, order, fetch_count, row_count):
                    if k in (1, 2):
                        if k == 1:
                            wait(dve, agg_ready, GROUP * (q - 1))
                        build(q, p, k - 1)
                    if k == 3:
                        dve.wait_ge(fetched[p], fetch_count)
                        order.did(nc.vector.tensor_reduce(ends_cut[:, :], cuts[:, p, 0:P], AX.X, ALU.add))
                        order.settle()
                        order.did(nc.vector.tensor_scalar(ends[:, GROUP:2 * GROUP], tile_of[:, :], ends_cut[:, 0:1], None, ALU.mult))
                    if k == 10:
                        dve.wait_ge(looked_up, 4 * q + 4)
                        dve.wait_ge(gathered[r], row_count)
                        order.did(nc.vector.tensor_tensor(scan_a[:, :], LOOK[:, 0:P], a_edge[:, cols(P * q, P)], ALU.add))
                        order.settle()
                        order.did(nc.vector.tensor_tensor(scan_b[:, :].rearrange("p (t h) -> p t h", h=HEADS),
                                                          scan_a[:, :].rearrange("p (t h) -> p t h", h=HEADS),
                                                          rows[:, r, :, D:XROW], ALU.add))
                        order.settle()
                        nc.vector.scalar_tensor_tensor(out=logits[:, :], in0=scan_b[:, :], scalar=0.2, in1=scan_b[:, :],
                                                       op0=ALU.mult, op1=ALU.max).then_inc(logits_ready, 1)
                    if k == 11:
                        dve.wait_ge(vt_ready, q + 1)
                        order.did(nc.vector.tensor_tensor_scan(scan_a[:, :], cuts[:, p, 0:P], VT[:, 0:P], -BIG, ALU.add, ALU.max))
                        order.settle()
                        nc.vector.tensor_scalar(ends[:, 0:GROUP], tile_of[:, :], scan_a[:, P - 1:P], None, ALU.mult).then_inc(ends_ready, 1)
                    if k == 12:
                        dve.wait_ge(ends_turned, q + 1)
                        order.did(nc.vector.tensor_copy(ends_row[:, :], MS[0:HEADS, 0:2 * GROUP]))
                        order.settle()
                        nc.vector.tensor_tensor_scan(running[:, 1:GROUP + 1], ends_row[:, GROUP:2 * GROUP], ends_row[:, 0:GROUP],
                                                     running[:, 0:1], ALU.add, ALU.max).then_inc(running_ready, 1)
                    if k == 13:
                        dve.wait_ge(carry_ready, q + 1)
                        order.did(nc.vector.tensor_copy(running[:, 0:1], running[:, GROUP:GROUP + 1]))
                        order.did(nc.vector.tensor_tensor(picked[:, :], MS[:, 32:32 + GROUP], tile_of[:, :], ALU.mult))
                        order.settle()
                        order.did(nc.vector.tensor_reduce(carried[:, :], picked[:, :], AX.X, ALU.add))
                        order.settle()
                        order.did(nc.vector.tensor_tensor_scan(scan_b[:, :], cuts[:, p, 0:P], VT[:, 0:P], carried[:, 0:1], ALU.add, ALU.max))
                        order.settle()
                        order.did(nc.vector.tensor_tensor_scan(scan_a[:, ::-1], cuts[:, p, P:0:-1], scan_b[:, ::-1], -BIG, ALU.add, ALU.max))
                        order.settle()
                        order.did(nc.vector.tensor_tensor(below[:, 0:P], VT[:, 0:P], scan_a[:, :], ALU.subtract))
                        order.did(nc.vector.tensor_tensor(picked[:, 0:1], carried[:, 0:1], cuts[:, p, 0:1], ALU.add))
                        order.settle()
                        nc.vector.tensor_tensor(below[:, P:P + 1], picked[:, 0:1], scan_a[:, 0:1], ALU.subtract).then_inc(below_ready, 1)
                    if k == 15:
                        dve.wait_ge(powers_ready, q + 1)
                        nc.vector.tensor_scalar(factors[:, :], tile_of[:, :], powers[:, P:P + 1], None, ALU.mult).then_inc(factors_ready, 1)

                def finish_front(q, p):
                    dve.wait_ge(weight_turned, q + 1)
                    nc.vector.tensor_copy(weight[:, p, :], MS[:, P:P + P + 3 * GROUP]).then_inc(weight_ready, 1)

                def weigh(s, u, p, g):
                    v = rows[:, u, 4 * g:4 * (g + 1), 0:D].rearrange("p t (h c) -> p t h c", c=C)
                    w = weight[:, p, 4 * HEADS * g:4 * HEADS * (g + 1)].rearrange("p (t h) -> p t h", h=HEADS)
                    nc.vector.tensor_tensor(v, v, w.unsqueeze(3).to_broadcast([P, 4, HEADS, C]), ALU.mult).then_inc(weighted, 1)

                def group(s, u, i):
                    p = u % 2
                    bases = tile_bases(nc, base_row, ENGINE.DVE, GROUP * s)
                    order = Order(dve, steps, NSTEP * (s + 1) + 1)
                    finish_front(s, p)
                    dve.wait_ge(weight_ready, s + 1)
                    weigh(s, u, p, 0)
                    if more(s, 4):
                        nc.vector.tensor_copy(idx[:, u, :], srcT[:, cols(GROUP * s + 4 * GROUP, GROUP)]).then_inc(idx_ready, 1)
                    weigh(s, u, p, 1)
                    for t in range(GROUP):
                        if t in (4, 8):
                            weigh(s, u, p, t // 4 + 1)
                        if more(s):
                            front(s + 1, 1 - p, (u + 1) % 4, t, order, fetches(s, u, i), 16 * GROUP * (i + (u + 1) // 4 + 1))
                        col = acc[:, :, bass.ds(bases[t], 1)].rearrange("p a o -> p (a o)")
                        now = AGG[t % 4][:, 0:3 * P].rearrange("p (a b) -> p a b", a=3)[:, :, 0]
                        fac = weight[:, p, P:P + 3 * GROUP].rearrange("p (a b) -> p a b", a=3)[:, :, t]
                        wait(dve, acc_copied, GROUP * s + t)
                        wait(dve, agg_free, GROUP * s + t)
                        nc.vector.tensor_tensor(col, col, fac, ALU.mult).then_inc(scaled, 1)
                        dve.wait_ge(acc_copied, GROUP * s + t + 1)
                        dve.wait_ge(scaled, GROUP * s + t + 1)
                        nc.vector.tensor_tensor(col, col, now, ALU.add).then_inc(agg_free, 1)
                    if more(s):
                        assert order.steps == NSTEP, order.steps

                nc.vector.memset(running[:, 0:1], -BIG).then_inc(steps, 1)
                dve.wait_ge(steps, 1)
                for r in range(4):
                    nc.vector.tensor_copy(idx[:, r, :], srcT[:, GROUP * r:GROUP * (r + 1)]).then_inc(idx_ready, 1)
                order = Order(dve, steps, 1)
                for k in range(GROUP):
                    front(0, 0, 0, k, order, FETCHES, 16 * GROUP)
                assert order.steps == NSTEP
                fours(dve, group)

        taken[0] = 0
        x1_in, staged3 = carve(2, D), carve(2, 3 * P)
        x1_bias, x1_beta, y1, t1, g1, y2, result = (carve(2, D) for _ in range(7))
        bias_all, gamma_all, beta_all = carve(D), carve(D), carve(D)
        stats, moments, spreads = carve(2, 6), carve(2, 2), carve(2, 4)
        stats2, moments2, spreads2 = carve(2, 6), carve(2, 2), carve(2, 4)
        rden = carve(2, HEADS)

        with ExitStack() as phase:
            def psem(name):
                return phase.enter_context(nc.semaphore(name))
            vectors = psem("vectors_loaded")
            x1_loaded = [psem(f"x1_loaded{p}") for p in range(2)]
            staged_ready, sums_turned = psem("sums_staged"), psem("sums_turned")
            x1_added = psem("x1_added")
            y1_made, var1_ready, sd1_ready = psem("y1_made"), psem("var1_ready"), psem("sd1_ready")
            t1_made, g1_made = psem("t1_made"), psem("g1_made")
            y2_made, var2_ready, sd2_ready, result_made = psem("y2_made"), psem("var2_ready"), psem("sd2_ready"), psem("result_made")
            stored = [psem(f"stored{p}") for p in range(2)]
            den_ready, rden_ready, y1_added = psem("den_ready"), psem("rden_ready"), psem("y1_added")
            stats1_made, moments1_made, rsd1_made = psem("stats1_made"), psem("moments1_made"), psem("rsd1_made")
            stats2_made, moments2_made, rsd2_made = psem("stats2_made"), psem("moments2_made"), psem("rsd2_made")
            gate = psem("final_gate")
            block = phase.enter_context(nc.Block())

            @block.sync
            def _(sp):
                for v, a in ((bias_all, bias), (gamma_all, gamma), (beta_all, beta)):
                    sp.dma_start(v, a.partition_broadcast(P)).then_inc(vectors, 16)

                def step(j, u, half):
                    if inside(j):
                        wait(sp, x1_added, j - 1)
                        sp.dma_start(x1_in[:, u, :], x1_dram[cols(j * P, P), :]).then_inc(x1_loaded[u], 16)
                    if inside(j - 3):
                        sp.wait_ge(result_made, j - 2)
                        n = last_rows if isinstance(j, int) and j - 3 == BLOCKS - 1 else P
                        sp.dma_start(out[cols((j - 3) * P, n), :], result[0:n, 1 - u, :]).then_inc(stored[1 - u], 16)
                skewed(sp, step, 3)
                for p in range(2):
                    sp.wait_ge(stored[p], 16 * (25 - p))

            @block.gpsimd
            def _(pool):
                pool.wait_ge(vectors, 48)

                def step(j, u, half):
                    if inside(j):
                        pool.wait_ge(x1_loaded[u], 16 * (half(0) + 1))
                        wait(pool, y2_made, j - 1)
                        nc.gpsimd.tensor_tensor(x1_bias[:, u, :], x1_in[:, u, :], bias_all, ALU.add)
                        nc.gpsimd.tensor_tensor(x1_beta[:, u, :], x1_in[:, u, :], beta_all, ALU.add).then_inc(x1_added, 1)
                    if inside(j - 1):
                        pool.wait_ge(t1_made, j)
                        wait(pool, y2_made, j - 2)
                        nc.gpsimd.tensor_tensor(g1[:, 1 - u, :], t1[:, 1 - u, :], gamma_all, ALU.mult).then_inc(g1_made, 1)
                skewed(pool, step, 3)

            @block.tensor
            def _(pe):
                def step(j, u, half):
                    if inside(j):
                        pe.wait_ge(staged_ready, j + 1)
                        wait(pe, y1_made, j - 1)
                        for k in range(3):
                            last = nc.tensor.transpose(PS[u][:, P * k:P * (k + 1)], staged3[:, u, P * k:P * (k + 1)], ident[:, :])
                        last.then_inc(sums_turned, 1)
                skewed(pe, step, 3)

            @block.scalar
            def _(act):
                def step(j, u, half):
                    if inside(j):
                        wait(act, sums_turned, j - 1)
                        act.sem_inc(gate, 1)
                        nc.scalar.copy(staged3[:, u, :].rearrange("p (k n) -> p k n", k=3),
                                       acc[:, :, cols(j * P, P)]).then_inc(staged_ready, 1)
                    if inside(j):
                        act.wait_ge(var1_ready, j + 1)
                        nc.scalar.activation(spreads[:, u, 1:2], spreads[:, u, 0:1], ACT.Sqrt).then_inc(sd1_ready, 1)
                    if inside(j - 2):
                        act.wait_ge(var2_ready, j - 1)
                        nc.scalar.activation(spreads2[:, u, 1:2], spreads2[:, u, 0:1], ACT.Sqrt).then_inc(sd2_ready, 1)
                skewed(act, step, 3)

            @block.vector
            def _(dve):
                def step(j, u, half):
                    v = 1 - u
                    if inside(j - 1):
                        dve.wait_ge(sd1_ready, j)
                        nc.vector.reciprocal(spreads[:, v, 2:3], spreads[:, v, 1:2]).then_inc(rsd1_made, 1)
                        dve.wait_ge(rsd1_made, j)
                        wait(dve, g1_made, j - 2)
                        nc.vector.tensor_scalar(t1[:, v, :], y1[:, v, :], moments[:, v, 0:1], spreads[:, v, 2:3],
                                                ALU.subtract, ALU.mult).then_inc(t1_made, 1)
                    if inside(j - 3):
                        dve.wait_ge(sd2_ready, j - 2)
                        nc.vector.reciprocal(spreads2[:, v, 2:3], spreads2[:, v, 1:2]).then_inc(rsd2_made, 1)
                        dve.wait_ge(rsd2_made, j - 2)
                        wait(dve, stored[v], 16 * half(3))
                        nc.vector.tensor_scalar(result[:, v, :], y2[:, v, :], moments2[:, v, 0:1], spreads2[:, v, 2:3],
                                                ALU.subtract, ALU.mult).then_inc(result_made, 1)
                    if inside(j - 2):
                        dve.wait_ge(g1_made, j - 1)
                        nc.vector.tensor_tensor(y2[:, u, :], g1[:, u, :], x1_beta[:, u, :], ALU.add).then_inc(y2_made, 1)
                        dve.wait_ge(y2_made, j - 1)
                        nc.vector.bn_stats(stats2[:, u, :], y2[:, u, :]).then_inc(stats2_made, 1)
                        dve.wait_ge(stats2_made, j - 1)
                        dve.sem_inc(gate, 1)
                        nc.vector.bn_aggr(moments2[:, u, :], stats2[:, u, :]).then_inc(moments2_made, 1)
                        dve.wait_ge(moments2_made, j - 1)
                        nc.vector.tensor_scalar(spreads2[:, u, 0:1], moments2[:, u, 1:2], LN_EPS, None, ALU.add).then_inc(var2_ready, 1)
                    if inside(j):
                        dve.wait_ge(sums_turned, j + 1)
                        nc.vector.tensor_scalar(rden[:, u, :], PS[u][:, 2 * P:2 * P + HEADS], 1.0e-16, None, ALU.add).then_inc(den_ready, 1)
                        dve.wait_ge(den_ready, j + 1)
                        nc.vector.reciprocal(rden[:, u, :], rden[:, u, :]).then_inc(rden_ready, 1)
                        dve.wait_ge(rden_ready, j + 1)
                        nc.vector.tensor_tensor(y1[:, u, :].rearrange("p (h c) -> p h c", c=C),
                                                PS[u][:, 0:D].rearrange("p (h c) -> p h c", c=C),
                                                rden[:, u, :].unsqueeze(2).to_broadcast([P, HEADS, C]), ALU.mult).then_inc(y1_made, 1)
                        dve.wait_ge(y1_made, j + 1)
                        dve.wait_ge(x1_added, j + 1)
                        nc.vector.tensor_tensor(y1[:, u, :], y1[:, u, :], x1_bias[:, u, :], ALU.add).then_inc(y1_added, 1)
                        dve.wait_ge(y1_added, j + 1)
                        nc.vector.bn_stats(stats[:, u, :], y1[:, u, :]).then_inc(stats1_made, 1)
                        dve.wait_ge(stats1_made, j + 1)
                        dve.sem_inc(gate, 1)
                        nc.vector.bn_aggr(moments[:, u, :], stats[:, u, :]).then_inc(moments1_made, 1)
                        dve.wait_ge(moments1_made, j + 1)
                        nc.vector.tensor_scalar(spreads[:, u, 0:1], moments[:, u, 1:2], LN_EPS, None, ALU.add).then_inc(var1_ready, 1)
                skewed(dve, step, 3)


_INS = ['x', 'src', 'dst', 'edge_attr_64', 'L0_gnn_W', 'L0_gnn_b', 'L1_gnn_W', 'L1_gnn_W_e', 'L1_gnn_att_src', 'L1_gnn_att_dst',
        'L1_gnn_att_edge', 'L1_gnn_bias', 'L1_gnn_gamma', 'L1_gnn_beta']


def kernel(**inputs):
    import numpy as _np
    import concourse.bacc as _bacc
    from concourse import mybir as _mybir
    from concourse.bass_utils import run_bass_kernel_spmd as _run

    nc = _bacc.Bacc("TRN2", target_bir_lowering=False, num_devices=1)
    arrays, args = {}, []
    for name in _INS:
        a = _np.ascontiguousarray(inputs[name])
        arrays[f"in_{name}"] = a
        args.append(nc.dram_tensor(f"in_{name}", a.shape, _mybir.dt.from_np(a.dtype), kind="ExternalInput").ap())
    args.append(nc.dram_tensor("out_0", (N, D), _mybir.dt.float32, kind="ExternalOutput").ap())
    gnn_kernel(nc, *args)
    r = _run(nc, [arrays], core_ids=[0])
    return r.results[0]["out_0"]
```

```python
import concourse.bass as bass
from concourse import mybir
from contextlib import ExitStack

P = 128
N, D, E, EDIM = 6250, 256, 106250, 64
HEADS = 8
C = D // HEADS
GROUP = 16
GROUPS = -(-E // (P * GROUP))
TILES = GROUP * GROUPS
BLOCKS = -(-N // P)
CHUNKS = 7
ROWS = CHUNKS * P
ACC = BLOCKS * P + P
XROW = D + HEADS
WIDE = XROW + HEADS
FULL, LEFT = E // P, E % P
WINDOW = 32
BIG = 1.0e30
LN_EPS = 1.0e-5

fp32 = mybir.dt.float32
i32 = mybir.dt.int32
ALU = mybir.AluOpType
ACT = mybir.ActivationFunctionType
AX = mybir.AxisListType
ENGINE = mybir.EngineType


def wait(engine, semaphore, value):
    if isinstance(value, int) and value <= 0:
        return
    engine.wait_ge(semaphore, value)


class Order:

    def __init__(self, engine, semaphore, start):
        self.engine, self.semaphore, self.start, self.steps = engine, semaphore, start, 0

    def did(self, instruction):
        instruction.then_inc(self.semaphore, 1)
        self.steps += 1

    def settle(self):
        wait(self.engine, self.semaphore, self.start + self.steps)


def cols(start, size):
    return bass.ds(start, size) if not isinstance(start, int) else slice(start, start + size)


def tile_bases(nc, base_row, engine, first_tile):
    _, values = nc.values_load_multi_w_load_instructions(
        base_row[0:1, cols(first_tile, GROUP)], engines=(engine,), min_val=0, max_val=N,
        skip_runtime_bounds_check_because="they are node numbers, at most N for the padding")
    return values


def gnn_kernel(nc, x, src, dst, edge_attr, w0, b0, w1, w_e, att_src, att_dst, att_edge, bias, gamma, beta, out):
    ctx = ExitStack()
    with ctx:
        def sb(name, shape, dt=fp32):
            return ctx.enter_context(nc.sbuf_tensor(name, shape, dt))

        def sem(name):
            return ctx.enter_context(nc.semaphore(name))

        z_dram = nc.dram_tensor("z_dram", (BLOCKS * P, D), fp32).ap()
        x1_dram = nc.dram_tensor("x1_dram", (BLOCKS * P, D), fp32).ap()
        xp_dram = nc.dram_tensor("xp_dram", (BLOCKS * P, XROW), fp32).ap()
        adst_dram = nc.dram_tensor("adst_dram", (ACC, HEADS), fp32).ap()
        max_dram = nc.dram_tensor("max_dram", (ACC, HEADS), fp32).ap()
        bases_dram = nc.dram_tensor("bases_dram", (1, ROWS), i32).ap()
        cut_dram = nc.dram_tensor("cut_dram", (ROWS * P,), fp32)

        gate = sem("gate")
        PS = [ctx.enter_context(nc.psum_tensor(f"bank{i}", [P, 512], fp32)) for i in range(8)]

        acc = sb("acc", [P, 3, ACC])
        srcT = sb("srcT", [P, ROWS], i32)
        relT = sb("relT", [P, ROWS])
        base_row = sb("base_row", [1, ROWS], i32)
        flag = sb("flag", [1, 1], i32)
        a_edge = sb("a_edge", [P, TILES * HEADS])
        ident = sb("ident", [P, P])
        iota = sb("iota", [P, P])
        head_of = sb("head_of", [P, HEADS])
        tile_of = sb("tile_of", [P, GROUP])
        spread = sb("spread", [P, 3, P])

        region = sb("region", [P, 4 * GROUP * XROW])
        taken = [0]

        def carve(*shape):
            size = 1
            for n in shape:
                size *= n
            v = region[:, taken[0]:taken[0] + size]
            taken[0] += size
            if len(shape) == 2:
                v = v.rearrange("p (a b) -> p a b", a=shape[0])
            if len(shape) == 3:
                v = v.rearrange("p (a b c) -> p a b c", a=shape[0], b=shape[1])
            return v

        w_self = carve(2, D)
        w_agg = carve(2, D)
        w_wide = carve(2, WIDE)
        b0_all = carve(D)
        v_edge = carve(2 * HEADS)
        ones = carve(P)
        rdeg = carve(BLOCKS)
        contB = carve(ROWS)
        shared = taken[0]

        dcur = carve(CHUNKS, P)
        dprev = carve(CHUNKS, P)
        srcf = carve(CHUNKS, P)
        diff = carve(CHUNKS, P)
        cut = carve(CHUNKS, P)
        rel = carve(CHUNKS, P)
        cont = carve(CHUNKS)
        jumps = carve(CHUNKS, P)
        jumped, jumps_all, is_sorted = carve(1), carve(1), carve(1)
        w0_in = carve(2, 2 * D)
        w1_in = carve(2, D)
        we_in = carve(D)
        att_b = carve(3, D)
        prod = carve(3, D)
        ints = region[:, taken[0]:taken[0] + 3 * ROWS].bitcast(i32).rearrange("p (a c e) -> p a c e", a=3, c=CHUNKS)
        taken[0] += 3 * ROWS
        assert taken[0] <= 4 * GROUP * XROW, taken[0]

        with ExitStack() as phase:
            blank = phase.enter_context(nc.semaphore("index_blank"))
            loaded = phase.enter_context(nc.semaphore("index_loaded"))
            weights = phase.enter_context(nc.semaphore("weights_loaded"))
            made = phase.enter_context(nc.semaphore("constants_made"))
            cast = phase.enter_context(nc.semaphore("vector_steps"))
            turned = phase.enter_context(nc.semaphore("indices_turned"))
            wturned = phase.enter_context(nc.semaphore("weights_turned"))
            stored = phase.enter_context(nc.semaphore("cuts_stored"))
            flagged = phase.enter_context(nc.semaphore("jumps_summed"))
            maskt = phase.enter_context(nc.semaphore("masks_turned"))
            block = phase.enter_context(nc.Block())
            SRC, CUR, PREV = range(3)
            CASTS = 6

            @block.gpsimd
            def _(pool):
                nc.gpsimd.memset(ints[:, SRC, :, :], 0)
                nc.gpsimd.memset(ints[:, CUR, :, :], N)
                nc.gpsimd.memset(ints[:, PREV, :, :], N).then_inc(blank, 1)
                pool.wait_ge(blank, 1)
                nc.gpsimd.memset(ints[0:1, PREV, 0, 0:1], -1).then_inc(blank, 1)
                nc.gpsimd.memset(ones, 1.0)
                nc.gpsimd.memset(v_edge, 0.0)
                nc.gpsimd.iota(iota[:, :], [[1, P]], base=0, channel_multiplier=0,
                               allow_small_or_imprecise_dtypes=True)
                nc.gpsimd.memset(ident[:, :], 0.0).then_inc(made, 1)
                pool.wait_ge(made, 1)
                nc.gpsimd.affine_select(out=ident[:, :], in_=ident[:, :], compare_op=ALU.not_equal, fill=1.0,
                                        base=0, pattern=[[-1, P]], channel_multiplier=1).then_inc(made, 1)
                nc.gpsimd.memset(acc[:, :, :], 0.0).then_inc(made, 1)

            @block.sync
            def _(sp):
                sp.wait_ge(blank, 2)
                whole = 6 * P * P
                rest = FULL - 6 * P

                for which, array in ((SRC, src), (CUR, dst)):
                    sp.dma_start(ints[:, which, 0:6, :], array[0:whole].rearrange("(c t e) -> t c e", c=6, e=P)).then_inc(loaded, 16)
                    sp.dma_start(ints[0:rest, which, 6, :], array[whole:FULL * P].rearrange("(t e) -> t e", e=P)).then_inc(loaded, 16)
                    sp.dma_start(ints[rest:rest + 1, which, 6, 0:LEFT], array[FULL * P:E].rearrange("(t e) -> t e", t=1)).then_inc(loaded, 16)
                sp.dma_start(ints[0:1, PREV, 0, 1:P], dst[0:P - 1].rearrange("(t e) -> t e", t=1)).then_inc(loaded, 16)
                sp.dma_start(ints[1:P, PREV, 0, :], dst[P - 1:P - 1 + (P - 1) * P].rearrange("(t e) -> t e", e=P)).then_inc(loaded, 16)
                sp.dma_start(ints[:, PREV, 1:6, :], dst[P * P - 1:whole - 1].rearrange("(c t e) -> t c e", c=5, e=P)).then_inc(loaded, 16)
                sp.dma_start(ints[0:rest, PREV, 6, :], dst[whole - 1:FULL * P - 1].rearrange("(t e) -> t e", e=P)).then_inc(loaded, 16)
                sp.dma_start(ints[rest:rest + 1, PREV, 6, 0:LEFT + 1], dst[FULL * P - 1:E].rearrange("(t e) -> t e", t=1)).then_inc(loaded, 16)
                sp.wait_ge(cast, CASTS)
                sp.dma_start(cut_dram.ap().rearrange("(c t e) -> t c e", c=CHUNKS, e=P), cut).then_inc(stored, 16)
                sp.wait_ge(maskt, 1)
                sp.dma_start(bases_dram[:, :], base_row[:, :]).then_inc(stored, 16)
                sp.wait_ge(stored, 32)

            @block.scalar
            def _(act):
                act.dma_start(w0_in, w0.rearrange("(k p) i -> p k i", p=P)).then_inc(weights, 16)
                act.dma_start(w1_in, w1.rearrange("(k p) o -> p k o", p=P)).then_inc(weights, 16)
                act.dma_start(we_in[0:EDIM, :], w_e[:, :]).then_inc(weights, 16)
                act.dma_start(we_in[EDIM:2 * EDIM, :], w_e[:, :]).then_inc(weights, 16)
                for n, att in enumerate((att_src, att_dst, att_edge)):
                    act.dma_start(att_b[:, n, :], att.rearrange("h c -> (h c)").partition_broadcast(P)).then_inc(weights, 16)
                act.dma_start(b0_all, b0.partition_broadcast(P)).then_inc(weights, 16)
                act.wait_ge(turned, 1)
                for n in range(2):
                    width = 4 * P if n == 0 else 3 * P
                    nc.scalar.copy(relT[:, 4 * P * n:4 * P * n + width], PS[n][:, 0:width])
                    nc.scalar.copy(srcT[:, 4 * P * n:4 * P * n + width], PS[2 + n][:, 0:width])
                    nc.scalar.copy(contB[:, 4 * P * n:4 * P * n + width], PS[4 + n][:, 0:width])
                    nc.scalar.copy(base_row[0:1, 4 * P * n:4 * P * n + width], PS[6 + n][0:1, 0:width])
                act.drain().then_inc(maskt, 1)
                act.wait_ge(wturned, 1)
                nc.scalar.copy(w_self[:, :, :].rearrange("p a b -> p (a b)"), PS[0][:, :])
                nc.scalar.copy(w_agg[:, :, :].rearrange("p a b -> p (a b)"), PS[1][:, :])

            @block.vector
            def _(dve):
                order = Order(dve, cast, 0)
                dve.wait_ge(loaded, 16 * 11)
                order.did(nc.vector.tensor_copy(srcf, ints[:, SRC, :, :]))
                order.did(nc.vector.tensor_copy(dcur, ints[:, CUR, :, :]))
                order.did(nc.vector.tensor_copy(dprev, ints[:, PREV, :, :]))
                order.settle()
                order.did(nc.vector.tensor_tensor(rel, dcur, dcur[:, :, 0:1].to_broadcast([P, CHUNKS, P]), ALU.subtract))
                order.did(nc.vector.tensor_tensor(diff, dcur, dprev, ALU.subtract))
                order.settle()
                order.did(nc.vector.tensor_scalar(cut, diff, 0.0, -BIG, ALU.not_equal, ALU.mult))
                assert order.steps == CASTS
                order.did(nc.vector.tensor_scalar(cont, diff[:, :, 0], 0.0, None, ALU.is_equal))
                order.did(nc.vector.scalar_tensor_tensor(out=jumps, in0=diff, scalar=-1.0, in1=diff, op0=ALU.add, op1=ALU.mult))
                order.settle()
                order.did(nc.vector.scalar_tensor_tensor(out=jumps, in0=rel, scalar=WINDOW - 1.0, in1=jumps, op0=ALU.is_gt, op1=ALU.add))
                order.settle()
                order.did(nc.vector.tensor_reduce(jumped, jumps.rearrange("p c e -> p (c e)"), AX.X, ALU.add))
                dve.wait_ge(made, 2)
                th = ident[:, :].rearrange("p (t h) -> p t h", h=HEADS)
                order.did(nc.vector.tensor_reduce(head_of[:, :], th.rearrange("p t h -> p h t"), AX.X, ALU.add))
                order.did(nc.vector.tensor_reduce(tile_of[:, :], th, AX.X, ALU.add))
                order.settle()
                for k in range(2):
                    order.did(nc.vector.tensor_copy(spread[:, k, :].rearrange("p (h c) -> p h c", c=C),
                                                    head_of[:, 4 * k:4 * k + 4].unsqueeze(2).to_broadcast([P, 4, C])))
                order.did(nc.vector.tensor_copy(spread[:, 2, 0:HEADS], head_of[:, :]))
                order.did(nc.vector.memset(spread[:, 2, HEADS:P], 0.0))
                dve.wait_ge(weights, 16 * 8)
                order.did(nc.vector.tensor_copy(w_wide[:, :, 0:D], w1_in))
                order.did(nc.vector.tensor_tensor(prod[:, 2, :], we_in, att_b[:, 2, :], ALU.mult))
                for n in range(2):
                    for k in range(2):
                        order.settle()
                        order.did(nc.vector.tensor_tensor(prod[:, k, :], w1_in[:, k, :], att_b[:, n, :], ALU.mult))
                        order.settle()
                        order.did(nc.vector.tensor_reduce(w_wide[:, k, D + HEADS * n:D + HEADS * (n + 1)],
                                                          prod[:, k, :].rearrange("p (h c) -> p h c", c=C), AX.X, ALU.add))
                for n in range(2):
                    half = slice(EDIM * n, EDIM * (n + 1))
                    order.did(nc.vector.tensor_reduce(v_edge[half, HEADS * n:HEADS * (n + 1)],
                                                      prod[half, 2, :].rearrange("p (h c) -> p h c", c=C), AX.X, ALU.add))
                dve.wait_ge(flagged, 1)
                order.did(nc.vector.tensor_scalar(jumps_all[0:1, :], PS[7][0:1, 0:1], 1.0, None, ALU.min))
                order.settle()
                order.did(nc.vector.tensor_copy(flag[:, :], jumps_all[0:1, :]))
                order.did(nc.vector.tensor_scalar(is_sorted[0:1, :], jumps_all[0:1, :], -1.0, 1.0, ALU.mult, ALU.add))
                order.settle()
                dve.wait_ge(stored, 32)
                order.did(nc.vector.tensor_scalar(base_row[:, :], base_row[:, :], is_sorted[0:1, 0:1], None, ALU.mult))
                order.settle()

            @block.tensor
            def _(pe):
                pe.wait_ge(made, 2)
                pe.wait_ge(cast, CASTS + 1)
                for c in range(CHUNKS):
                    at = slice(P * (c % 4), P * (c % 4) + P)
                    nc.tensor.transpose(PS[c // 4][:, at], rel[:, c, :], ident[:, :])
                    nc.tensor.transpose(PS[2 + c // 4][:, at], srcf[:, c, :], ident[:, :])
                    nc.tensor.matmul(PS[4 + c // 4][:, at], cont[:, c:c + 1].to_broadcast([P, P]), ident[:, :], start=True, stop=True)
                    last = nc.tensor.transpose(PS[6 + c // 4][0:1, at], dcur[:, c, 0:1], ident[:, :])
                last.then_inc(turned, 1)
                pe.wait_ge(maskt, 1)
                pe.wait_ge(cast, CASTS + 4)
                nc.tensor.matmul(PS[7][0:1, 0:1], jumped, ones[:, 0:1], start=True, stop=True).then_inc(flagged, 1)
                pe.wait_ge(weights, 16 * 8)
                for i in range(4):
                    for o in range(2):
                        last = nc.tensor.transpose(PS[i // 2][:, D * (i % 2) + P * o:D * (i % 2) + P * (o + 1)],
                                                   w0_in[:, o, P * i:P * (i + 1)], ident[:, :])
                last.then_inc(wturned, 1)

        taken[0] = shared
        HALF = GROUP // 2
        ring = carve(2, GROUP, D)
        onehot = sb("onehot", [P, 2 * GROUP, P])
        edge_in = carve(2, GROUP * EDIM)
        edgeT = carve(2, 512)
        x_in = carve(2, D)
        xT = carve(2, D)
        z_out = carve(2, D)
        idx = sb("idx", [P, 4, GROUP], i32)
        assert taken[0] <= 4 * GROUP * XROW, taken[0]
        AGG = PS[0:4]
        TE, AE, ZB = PS[4:6], PS[6], PS[7]
        last_rows = N - (BLOCKS - 1) * P

        with ExitStack() as phase:
            def psem(name):
                return phase.enter_context(nc.semaphore(name))
            idx_ready = psem("idx0_ready")
            gathered = [[psem(f"gathered0_{p}{h}") for h in range(2)] for p in range(2)]
            onehot_ready = psem("onehot0_ready")
            agg_ready = psem("agg0_ready")
            acc_copied = psem("acc0_copied")
            agg_free = psem("agg0_free")
            edges_in = [psem(f"edges_in{p}") for p in range(2)]
            te_ready, te_copied = psem("te_ready"), psem("te_copied")
            ae_ready, ae_copied = psem("ae_ready"), psem("ae_copied")
            x_loaded = [psem(f"x_loaded{p}") for p in range(2)]
            xt_ready, xt_copied = psem("xt_ready"), psem("xt_copied")
            z_ready, z_summed = psem("z_ready"), psem("z_summed")
            z_stored = [psem(f"z_stored{p}") for p in range(2)]
            zeros_out = psem("adst_zeroed")
            xblank = psem("x_blank")
            zsum = psem("z_sum_steps")
            block = phase.enter_context(nc.Block())

            def pairs(engine, body):
                for u in range(2):
                    body(u, u, 0)
                with engine.Fori(1, 24) as i:
                    for u in range(2):
                        body(2 * i + u, u, i)
                for s in range(48, GROUPS):
                    body(s, s % 2, s // 2)

            def has_block(s):
                return not isinstance(s, int) or s < BLOCKS

            @block.gpsimd
            def _(pool):
                def group(s, u, i):
                    wait(pool, idx_ready, s + 1)
                    for h in range(2):
                        wait(pool, agg_ready, GROUP * (s - 2) + HALF * (h + 1))
                        pool.sem_inc(gate, 1)
                        for t in range(HALF * h, HALF * (h + 1)):
                            nc.gpsimd.indirect_dma_start(
                                out=ring[:, u, t, :], out_offset=None, in_=x[:, :],
                                in_offset=bass.IndirectOffsetOnAxis(ap=idx[:, u, t:t + 1], axis=0),
                            ).then_inc(gathered[u][h], 16)
                pairs(pool, group)

            @block.sync
            def _(sp):
                sp.wait_ge(xblank, 1)

                def load_edges(s, u):
                    if isinstance(s, int) and s == GROUPS - 1:
                        full = FULL - GROUP * s
                        sp.dma_start(edge_in[:, u, 0:full * EDIM].rearrange("p (t k) -> p t k", k=EDIM),
                                     edge_attr[GROUP * s * P:FULL * P, :].rearrange("(t p) k -> p t k", p=P)).then_inc(edges_in[u], 16)
                        sp.dma_start(edge_in[0:LEFT, u, full * EDIM:(full + 1) * EDIM],
                                     edge_attr[FULL * P:E, :]).then_inc(edges_in[u], 16)
                        return
                    sp.dma_start(edge_in[:, u, :].rearrange("p (t k) -> p t k", k=EDIM),
                                 edge_attr[cols(s * (GROUP * P), GROUP * P), :].rearrange("(t p) k -> p t k", p=P)).then_inc(edges_in[u], 16)

                def load_x(s, u):
                    n = last_rows if isinstance(s, int) and s == BLOCKS - 1 else P
                    sp.dma_start(x_in[0:n, u, :], x[cols(s * P, n), :]).then_inc(x_loaded[u], 16)

                def group(s, u, i):
                    if not isinstance(s, int) or s + 2 < GROUPS:
                        wait(sp, te_ready, 2 * s + 2)
                        load_edges(s + 2, u)
                    if has_block(s):
                        wait(sp, z_summed, s + 1)
                        sp.dma_start(z_dram[cols(s * P, P), :], z_out[:, u, :]).then_inc(z_stored[u], 16)
                    if not isinstance(s, int) or s + 2 < BLOCKS:
                        load_x(s + 2, u)

                for s in range(2):
                    load_edges(s, s)
                    load_x(s, s)

                sp.dma_start(adst_dram[BLOCKS * P:ACC, :], acc[:, 0, ACC - HEADS:ACC]).then_inc(zeros_out, 16)
                for u in range(2):
                    group(u, u, 0)
                with sp.Fori(1, 23) as i:
                    for u in range(2):
                        group(2 * i + u, u, i)
                for s in range(46, GROUPS):
                    group(s, s % 2, s // 2)
                sp.wait_ge(zeros_out, 16)
                sp.wait_ge(z_stored[0], 16 * 25)
                sp.wait_ge(z_stored[1], 16 * 24)

            @block.tensor
            def _(pe):
                def transposes(s, u, i, bank):
                    if bank == 0:
                        extra = 16 if isinstance(s, int) and s == GROUPS - 1 else 0
                        pe.wait_ge(edges_in[u], 16 * (i + 1) + extra)
                    wait(pe, te_copied, 2 * (s - 1) + bank + 1)
                    for j in range(4):
                        last = nc.tensor.transpose(TE[bank][:, P * j:P * (j + 1)],
                                                   edge_in[:, u, P * (4 * bank + j):P * (4 * bank + j + 1)], ident[:, :])
                    last.then_inc(te_ready, 1)

                def edge_products(s, u, bank):
                    pe.wait_ge(te_copied, 2 * s + bank + 1)
                    if bank == 0:
                        wait(pe, ae_copied, s)
                    for j in range(4):
                        q = 4 * bank + j
                        last = nc.tensor.matmul(AE[:, 16 * q:16 * (q + 1)], edgeT[:, bank, P * j:P * (j + 1)], v_edge,
                                                start=True, stop=True)
                    if bank == 1:
                        last.then_inc(ae_ready, 1)

                def group(s, u, i):
                    transposes(s, u, i, 0)
                    if has_block(s):
                        pe.wait_ge(x_loaded[u], 16 * (i + 1))
                        wait(pe, z_summed, s)
                        for k in range(2):
                            last = nc.tensor.transpose(ZB[:, P * k:P * (k + 1)], x_in[:, u, P * k:P * (k + 1)], ident[:, :])
                        last.then_inc(xt_ready, 1)
                    for t in range(GROUP):
                        if t == 3:
                            transposes(s, u, i, 1)
                        if t == 6:
                            edge_products(s, u, 0)
                        if t == 8 and has_block(s):
                            pe.wait_ge(xt_copied, s + 1)
                            for k in range(2):
                                last = nc.tensor.matmul(ZB[:, D:2 * D], xT[:, u, P * k:P * (k + 1)], w_self[:, k, :],
                                                        start=(k == 0), stop=(k == 1))
                            last.then_inc(z_ready, 1)
                        if t == 11:
                            edge_products(s, u, 1)
                        if t % HALF == 0:
                            pe.wait_ge(gathered[u][t // HALF], 16 * HALF * (i + 1))
                            pe.wait_ge(onehot_ready, 2 * s + t // HALF + 1)
                        wait(pe, agg_free, GROUP * s + t - 3)
                        hot = onehot[:, t, :]
                        bank = AGG[t % 4]
                        for k in range(2):
                            nc.tensor.matmul(bank[:, P * k:P * (k + 1)], ring[:, u, t, P * k:P * (k + 1)], hot, start=True, stop=True)
                        nc.tensor.matmul(bank[:, 2 * P:3 * P], ones[:, :], hot, start=True, stop=True).then_inc(agg_ready, 1)
                pairs(pe, group)

            @block.scalar
            def _(act):
                def group(s, u, i):
                    bases = tile_bases(nc, base_row, ENGINE.Activation, GROUP * s)
                    for t in range(GROUP):
                        if t == 1 and has_block(s):
                            act.wait_ge(xt_ready, s + 1)
                            wait(act, z_ready, s - 1)
                            nc.scalar.copy(xT[:, u, :], ZB[:, 0:D]).then_inc(xt_copied, 1)
                        act.wait_ge(agg_ready, GROUP * s + t + 1)
                        wait(act, acc_copied, GROUP * s + t)
                        act.sem_inc(gate, 1)
                        nc.scalar.copy(acc[:, :, bass.ds(bases[t] + 1, P - 1)],
                                       AGG[t % 4][:, 0:3 * P].rearrange("p (a b) -> p a b", a=3)[:, :, 1:P]).then_inc(acc_copied, 1)
                pairs(act, group)

            @block.vector
            def _(dve):
                def build_onehot(rel_cols, h):
                    nc.vector.tensor_tensor(onehot[:, HALF * h:HALF * (h + 1), :],
                                            iota[:, :].unsqueeze(1).to_broadcast([P, HALF, P]),
                                            rel_cols.unsqueeze(2).to_broadcast([P, HALF, P]), ALU.is_equal).then_inc(onehot_ready, 1)

                def group(s, u, i):
                    bases = tile_bases(nc, base_row, ENGINE.DVE, GROUP * s)
                    for t in range(GROUP):
                        if t == 0:
                            wait(dve, agg_ready, GROUP * s)
                            build_onehot(relT[:, cols(GROUP * s + HALF, HALF)], 1)
                        if t == 2 and (not isinstance(s, int) or s + 2 < GROUPS):
                            dve.wait_ge(gathered[u][1], 16 * HALF * (i + 1))
                            nc.vector.tensor_copy(idx[:, u, :], srcT[:, cols(GROUP * s + 2 * GROUP, GROUP)]).then_inc(idx_ready, 1)
                        if t == 1 or t == 5:
                            bank = t // 4
                            dve.wait_ge(te_ready, 2 * s + bank + 1)
                            nc.vector.tensor_copy(edgeT[:, bank, :], TE[bank][:, :]).then_inc(te_copied, 1)
                        if t == 9 and (not isinstance(s, int) or s + 1 < GROUPS):
                            dve.wait_ge(agg_ready, GROUP * s + HALF)
                            build_onehot(relT[:, cols(GROUP * s + GROUP, HALF)], 0)
                        if t == 11 and has_block(s):
                            dve.wait_ge(z_ready, s + 1)
                            wait(dve, z_stored[u], 16 * i)
                            nc.vector.tensor_tensor(z_out[:, u, :], ZB[:, D:2 * D], x_in[:, u, :], ALU.add).then_inc(zsum, 1)
                            dve.wait_ge(zsum, s + 1)
                            nc.vector.tensor_tensor(z_out[:, u, :], z_out[:, u, :], b0_all, ALU.add).then_inc(z_summed, 1)
                        if t == 14:
                            dve.wait_ge(ae_ready, s + 1)
                            nc.vector.tensor_copy(a_edge[:, cols(P * s, P)], AE[:, 0:P]).then_inc(ae_copied, 1)
                        dve.wait_ge(acc_copied, GROUP * s + t + 1)
                        wait(dve, agg_free, GROUP * s + t)
                        col = acc[:, :, bass.ds(bases[t], 1)].rearrange("p a o -> p (a o)")
                        nc.vector.scalar_tensor_tensor(
                            out=col, in0=col, scalar=contB[:, cols(GROUP * s + t, 1)],
                            in1=AGG[t % 4][:, 0:3 * P].rearrange("p (a b) -> p a b", a=3)[:, :, 0],
                            op0=ALU.mult, op1=ALU.add).then_inc(agg_free, 1)

                nc.vector.memset(x_in[:, :, :], 0.0).then_inc(xblank, 1)
                for s in range(2):
                    nc.vector.tensor_copy(idx[:, s, :], srcT[:, GROUP * s:GROUP * (s + 1)]).then_inc(idx_ready, 1)
                build_onehot(relT[:, 0:HALF], 0)
                pairs(dve, group)
        SPAN = 400
        SPANS = ACC // SPAN
        assert SPANS * SPAN == ACC
        BASES = 4 * P

        class General:

            def __init__(self, phase, name, carve):
                def psem(what):
                    return phase.enter_context(nc.semaphore(f"{name}_{what}"))
                self.nodes, self.hot, self.row = carve(ACC), carve(ACC), carve(XROW)
                spare = onehot[:, :, :].rearrange("p t n -> p (t n)")
                self.bases_in, self.bases_f, self.dst_of, self.unit = \
                    spare[0:1, 3 * ROWS:4 * ROWS].bitcast(i32), spare[0:1, 0:ROWS], spare[:, ROWS:2 * ROWS], spare[:, 2 * ROWS:2 * ROWS + P]
                self.iota_ready, self.bases_ready, self.bases_spread = psem("nodes_ready"), psem("bases_ready"), psem("bases_spread")
                self.prepared, self.bases_loaded = psem("prepared"), psem("bases_loaded")
                self.indexed, self.loaded = psem("tile_indexed"), psem("tile_loaded")
                self.hot_ready, self.summed, self.added = psem("hot_ready"), psem("tile_summed"), psem("sums_added")

            def number_nodes(self):
                nc.gpsimd.iota(self.nodes, [[1, ACC]], base=0, channel_multiplier=0,
                               allow_small_or_imprecise_dtypes=True).then_inc(self.iota_ready, 1)

            def load_bases(self, pool):
                pool.dma_start(self.bases_in, bases_dram[:, :]).then_inc(self.bases_loaded, 16)

            def spread_bases(self, pe):
                pe.wait_ge(self.bases_ready, 1)
                for n in range(0, ROWS, BASES):
                    width = min(BASES, ROWS - n)
                    last = nc.tensor.matmul(PS[n // BASES][:, 0:width], self.unit[0:1, 0:P], self.bases_f[:, n:n + width],
                                            start=True, stop=True)
                last.then_inc(self.bases_spread, 1)

            def prepare(self, dve):
                nc.vector.memset(acc[:, :, :], 0.0)
                nc.vector.memset(self.unit, 1.0)
                dve.wait_ge(self.bases_loaded, 16)
                nc.vector.tensor_copy(self.bases_f, self.bases_in).then_inc(self.bases_ready, 1)
                dve.wait_ge(self.bases_spread, 1)
                for n in range(0, ROWS, BASES):
                    width = min(BASES, ROWS - n)
                    nc.vector.tensor_tensor(self.dst_of[:, n:n + width], relT[:, n:n + width], PS[n // BASES][:, 0:width],
                                            ALU.add).then_inc(self.prepared, 1)
                dve.wait_ge(self.prepared, 2)
                dve.sem_inc(self.added, 2)
                dve.wait_ge(self.iota_ready, 1)

            def index_tile(self, dve, t):
                dve.sem_inc(gate, 1)
                nc.vector.tensor_copy(idx[:, 0, 0:1], srcT[:, cols(t, 1)])
                nc.vector.tensor_copy(idx[:, 0, 1:2], self.dst_of[:, cols(t, 1)]).then_inc(self.indexed, 1)

            def gather(self, pool, target, table, which, semaphore):
                pool.sem_inc(gate, 1)
                nc.gpsimd.indirect_dma_start(
                    out=target, out_offset=None, in_=table,
                    in_offset=bass.IndirectOffsetOnAxis(ap=idx[:, 0, which:which + 1], axis=0)).then_inc(semaphore, 16)

            def mark_nodes(self, dve, t):
                nc.vector.tensor_scalar(self.hot, self.nodes, self.dst_of[:, cols(t, 1)], None, ALU.is_equal).then_inc(self.hot_ready, 1)

            def sum_tile(self, pe, t, counts):
                pe.wait_ge(self.hot_ready, t + 1)
                for c in range(SPANS):
                    pe.wait_ge(self.added, SPANS * t + c + 1)
                    hot = self.hot[:, SPAN * c:SPAN * (c + 1)]
                    banks = PS[3 * (c % 2):3 * (c % 2) + 3]
                    for k in range(2):
                        nc.tensor.matmul(banks[k][:, 0:SPAN], self.row[:, P * k:P * (k + 1)], hot, start=True, stop=True)
                    nc.tensor.matmul(banks[2][0:HEADS, 0:SPAN], counts, hot, start=True, stop=True).then_inc(self.summed, 1)

            def add_tile(self, dve, t):
                dve.wait_ge(self.added, SPANS * t + 2)
                for c in range(SPANS):
                    dve.wait_ge(self.summed, SPANS * t + c + 1)
                    at = slice(SPAN * c, SPAN * (c + 1))
                    banks = PS[3 * (c % 2):3 * (c % 2) + 3]
                    for k in range(2):
                        nc.vector.tensor_tensor(acc[:, k, at], acc[:, k, at], banks[k][:, 0:SPAN], ALU.add)
                    nc.vector.tensor_tensor(acc[0:HEADS, 2, at], acc[0:HEADS, 2, at], banks[2][0:HEADS, 0:SPAN],
                                            ALU.add).then_inc(self.added, 1)

        def is_general(engine):
            return engine.value_load(flag[0:1, 0:1], min_val=0, max_val=1)

        taken[0] = shared
        with ExitStack() as phase:
            g = General(phase, "general0", carve)
            block = phase.enter_context(nc.Block())

            @block.gpsimd
            def _(pool):
                with pool.If(is_general(pool) != 0):
                    g.load_bases(pool)
                    g.number_nodes()
                    with pool.Fori(0, TILES) as t:
                        pool.wait_ge(g.indexed, t + 1)
                        g.gather(pool, g.row[:, 0:D], x[:, :], 0, g.loaded)

            @block.tensor
            def _(pe):
                with pe.If(is_general(pe) != 0):
                    g.spread_bases(pe)
                    with pe.Fori(0, TILES) as t:
                        pe.wait_ge(g.loaded, 16 * t + 16)
                        g.sum_tile(pe, t, g.unit[:, 0:HEADS])

            @block.vector
            def _(dve):
                with dve.If(is_general(dve) != 0):
                    g.prepare(dve)
                    with dve.Fori(0, TILES) as t:
                        g.index_tile(dve, t)
                        g.mark_nodes(dve, t)
                        g.add_tile(dve, t)

        taken[0] = shared
        RING = 4
        z_in, staged, y_mid, x1_new, x1T = (carve(RING, D) for _ in range(5))
        x_wide = carve(RING, WIDE)
        stats, moments, spreads = carve(RING, 6), carve(RING, 2), carve(RING, 4)
        DEG = PS[6]
        UNROLL = 8

        def staggered(engine, body, lags):
            for j in range(2 * UNROLL):
                body(j, j % UNROLL, lambda lag, ring, j=j: (j - lag) // ring)
            with engine.Fori(2, BLOCKS // UNROLL) as i:
                for u in range(UNROLL):
                    body(UNROLL * i + u, u, lambda lag, ring, u=u: i * (UNROLL // ring) + (u - lag) // ring)
            for j in range(BLOCKS // UNROLL * UNROLL, BLOCKS + lags):
                body(j, j % UNROLL, lambda lag, ring, j=j: (j - lag) // ring)

        def inside(b):
            return not isinstance(b, int) or 0 <= b < BLOCKS

        def uses(r, ring):
            return (BLOCKS - r + ring - 1) // ring

        with ExitStack() as phase:
            def psem(name):
                return phase.enter_context(nc.semaphore(name))
            deg_ready, rdeg_steps = psem("degrees_ready"), psem("rdeg_steps")
            z_loaded = [psem(f"z_loaded{p}") for p in range(RING)]
            staged_ready, product_ready = psem("staged_ready"), psem("product_ready")
            y_made, var_ready, sd_ready = psem("y_made"), psem("var_ready"), psem("sd_ready")
            x1_ready, x1t_ready, x1t_copied = psem("x1_ready"), psem("x1t_ready"), psem("x1t_copied")
            wide_ready, wide_copied = psem("wide_ready"), psem("wide_copied")
            x1_stored = [psem(f"x1_stored{p}") for p in range(RING)]
            wide_stored = [psem(f"wide_stored{p}") for p in range(RING)]
            moment_steps, rsd_made = psem("moment_steps"), psem("rsd_made")
            PRODUCT, ADD, ROOT, NORM, TURN_X1, COPY_X1T, PROJECT, COPY_WIDE, STORE_WIDE = 1, 2, 2, 3, 3, 3, 4, 5, 5
            block = phase.enter_context(nc.Block())

            @block.sync
            def _(sp):
                def slot(j, u, turn):
                    if inside(j):
                        wait(sp, y_made, j - RING + 1)
                        r = u % RING
                        sp.dma_start(z_in[:, r, :], z_dram[cols(j * P, P), :]).then_inc(z_loaded[r], 16)
                    if inside(j - TURN_X1):
                        b, r = j - TURN_X1, (u - TURN_X1) % RING
                        sp.wait_ge(x1_ready, b + 1)
                        sp.dma_start(x1_dram[cols(b * P, P), :], x1_new[:, r, :]).then_inc(x1_stored[r], 16)
                    if inside(j - STORE_WIDE):
                        b, r = j - STORE_WIDE, (u - STORE_WIDE) % RING
                        sp.wait_ge(wide_copied, b + 1)
                        sp.dma_start(xp_dram[cols(b * P, P), :], x_wide[:, r, 0:XROW]).then_inc(wide_stored[r], 16)
                        sp.dma_start(adst_dram[cols(b * P, P), :], x_wide[:, r, XROW:WIDE]).then_inc(wide_stored[r], 16)
                staggered(sp, slot, STORE_WIDE)
                for r in range(RING):
                    sp.wait_ge(x1_stored[r], 16 * uses(r, RING))
                    sp.wait_ge(wide_stored[r], 32 * uses(r, RING))

            @block.tensor
            def _(pe):
                for b in range(BLOCKS):
                    last = nc.tensor.matmul(DEG[:, b:b + 1], acc[0:1, 2, P * b:P * (b + 1)], ones[0:1, 0:1], start=True, stop=True)
                last.then_inc(deg_ready, 1)

                def slot(j, u, turn):
                    if inside(j - PRODUCT):
                        b, v = j - PRODUCT, u - PRODUCT
                        pe.wait_ge(staged_ready, b + 1)
                        wait(pe, y_made, b - 1)
                        for k in range(2):
                            last = nc.tensor.matmul(PS[v % 2][:, 0:D], staged[:, v % RING, P * k:P * (k + 1)], w_agg[:, k, :],
                                                    start=(k == 0), stop=(k == 1))
                        last.then_inc(product_ready, 1)
                    if inside(j - PROJECT):
                        b, v = j - PROJECT, u - PROJECT
                        pe.wait_ge(x1t_copied, b + 1)
                        wait(pe, wide_copied, b - 1)
                        for k in range(2):
                            last = nc.tensor.matmul(PS[4 + v % 2][:, 0:WIDE], x1T[:, v % RING, P * k:P * (k + 1)], w_wide[:, k, :],
                                                    start=(k == 0), stop=(k == 1))
                        last.then_inc(wide_ready, 1)
                    if inside(j - TURN_X1):
                        b, v = j - TURN_X1, u - TURN_X1
                        pe.wait_ge(x1_ready, b + 1)
                        wait(pe, x1t_copied, b - 1)
                        for k in range(2):
                            last = nc.tensor.transpose(PS[2 + v % 2][:, P * k:P * (k + 1)], x1_new[:, v % RING, P * k:P * (k + 1)], ident[:, :])
                        last.then_inc(x1t_ready, 1)
                staggered(pe, slot, STORE_WIDE)

            @block.scalar
            def _(act):
                def slot(j, u, turn):
                    if inside(j):
                        wait(act, product_ready, j - RING + 1)
                        act.sem_inc(gate, 1)
                        nc.scalar.copy(staged[:, u % RING, :].rearrange("p (k n) -> p k n", k=2),
                                       acc[:, 0:2, cols(j * P, P)]).then_inc(staged_ready, 1)
                    if inside(j - COPY_X1T):
                        b, v = j - COPY_X1T, u - COPY_X1T
                        act.wait_ge(x1t_ready, b + 1)
                        wait(act, wide_ready, b - RING + 1)
                        nc.scalar.copy(x1T[:, v % RING, :], PS[2 + v % 2][:, 0:D]).then_inc(x1t_copied, 1)
                    if inside(j - ROOT):
                        b, r = j - ROOT, (u - ROOT) % RING
                        act.wait_ge(var_ready, b + 1)
                        nc.scalar.activation(spreads[:, r, 1:2], spreads[:, r, 0:1], ACT.Sqrt).then_inc(sd_ready, 1)
                staggered(act, slot, STORE_WIDE)

            @block.vector
            def _(dve):
                dve.wait_ge(deg_ready, 1)
                nc.vector.tensor_scalar(rdeg, DEG[:, 0:BLOCKS], 1.0, None, ALU.max).then_inc(rdeg_steps, 1)
                dve.wait_ge(rdeg_steps, 1)
                nc.vector.reciprocal(rdeg, rdeg).then_inc(rdeg_steps, 1)
                dve.wait_ge(rdeg_steps, 2)

                def slot(j, u, turn):
                    if inside(j - ADD):
                        b, v, r = j - ADD, u - ADD, (u - ADD) % RING
                        dve.wait_ge(product_ready, b + 1)
                        dve.wait_ge(z_loaded[r], 16 * turn(ADD, RING) + 16)
                        wait(dve, x1_ready, b - RING + 1)
                        dve.sem_inc(gate, 1)
                        nc.vector.scalar_tensor_tensor(out=y_mid[:, r, :], in0=PS[v % 2][:, 0:D], scalar=rdeg[:, cols(b, 1)],
                                                       in1=z_in[:, r, :], op0=ALU.mult, op1=ALU.add).then_inc(y_made, 1)
                    if inside(j - NORM):
                        b, r = j - NORM, (u - NORM) % RING
                        dve.wait_ge(sd_ready, b + 1)
                        nc.vector.reciprocal(spreads[:, r, 2:3], spreads[:, r, 1:2]).then_inc(rsd_made, 1)
                    if inside(j - ADD):
                        b, r = j - ADD, (u - ADD) % RING
                        dve.wait_ge(y_made, b + 1)
                        nc.vector.bn_stats(stats[:, r, :], y_mid[:, r, :]).then_inc(moment_steps, 1)
                    if inside(j - NORM):
                        b, r = j - NORM, (u - NORM) % RING
                        dve.wait_ge(rsd_made, b + 1)
                        wait(dve, x1_stored[r], 16 * turn(NORM, RING))
                        nc.vector.tensor_scalar(x1_new[:, r, :], y_mid[:, r, :], moments[:, r, 0:1], spreads[:, r, 2:3],
                                                ALU.subtract, ALU.mult).then_inc(x1_ready, 1)
                    if inside(j - ADD):
                        b, r = j - ADD, (u - ADD) % RING
                        dve.wait_ge(moment_steps, 2 * b + 1)
                        dve.sem_inc(gate, 1)
                        nc.vector.bn_aggr(moments[:, r, :], stats[:, r, :]).then_inc(moment_steps, 1)
                        dve.wait_ge(moment_steps, 2 * b + 2)
                        nc.vector.tensor_scalar(spreads[:, r, 0:1], moments[:, r, 1:2], LN_EPS, None, ALU.add).then_inc(var_ready, 1)
                    if inside(j - COPY_WIDE):
                        b, v, r = j - COPY_WIDE, u - COPY_WIDE, (u - COPY_WIDE) % RING
                        dve.wait_ge(wide_ready, b + 1)
                        wait(dve, wide_stored[r], 32 * turn(COPY_WIDE, RING))
                        nc.vector.tensor_copy(x_wide[:, r, :], PS[4 + v % 2][:, 0:WIDE]).then_inc(wide_copied, 1)
                staggered(dve, slot, STORE_WIDE)

        SLOTS = 4
        rows = region[:, :].rearrange("p (s t f) -> p s t f", s=SLOTS, t=GROUP)
        QUAD = P // WINDOW
        assert GROUP // QUAD == 4
        hot = onehot[:, 0:2 * GROUP * WINDOW // P, :].rearrange("p t n -> p (t n)").rearrange("p (s t w) -> p s t w", s=2, t=GROUP)
        hotT = sb("hotT", [P, 4 * P])
        windows = sb("windows", [P, 2, 4, QUAD * HEADS])
        cuts = sb("cuts", [P, 2, P + 1])
        logits = sb("logits", [P, P])
        scan_a = sb("scan_a", [P, P])
        scan_b = sb("scan_b", [P, P])
        below = scan_a
        powers = sb("powers", [P, P])
        weight = sb("weight", [P, 2, P])
        ends_cut = sb("ends_cut", [P, 1])
        ends = sb("ends", [P, 4 * GROUP])
        END, CUT_SUM, FIRST, CUT = (slice(GROUP * n, GROUP * (n + 1)) for n in range(4))
        ends_row = sb("ends_row", [HEADS, 4 * GROUP])
        running = sb("running", [HEADS, GROUP + 1])
        carry = sb("carry", [HEADS, GROUP])
        highest = sb("highest", [HEADS, GROUP])
        drop = sb("drop", [HEADS, 2 * GROUP])
        drop_exp = sb("drop_exp", [HEADS, 2 * GROUP])
        factor = sb("factor", [P, 2, 3, 2 * GROUP])
        fresh = sb("fresh", [P, 2, 3])
        AGG, TR, LOOK, CHAIN, TURN = PS[0:4], PS[4], PS[5], PS[6], PS[7]
        NSTEP = 12
        LAG = 2

        with ExitStack() as phase:
            def psem(name):
                return phase.enter_context(nc.semaphore(name))
            idx_ready = psem("idx1_ready")
            gathered = [psem(f"gathered1_{r}") for r in range(SLOTS)]
            fetched = [psem(f"windows_fetched{p}") for p in range(2)]
            hot_ready = psem("hot_ready")
            tr_ready, tr_copied = psem("tr_ready"), psem("tr_copied")
            looked_up = psem("looked_up")
            logits_ready, vt_ready = psem("logits_ready"), psem("vt_ready")
            below_ready, powers_ready = psem("below_ready"), psem("powers_ready")
            ends_ready, ends_turned = psem("ends_ready"), psem("ends_turned")
            drop_ready, drop_exp_ready = psem("drop_ready"), psem("drop_exp_ready")
            factors_spread, factors_ready = psem("factors_spread"), psem("factors_ready")
            weight_turned, weight_ready = psem("weight_turned"), psem("weight_ready")
            weighted = psem("rows_weighted")
            agg_ready, acc_copied, agg_free = psem("agg1_ready"), psem("acc1_copied"), psem("agg1_free")
            scaled = psem("column_scaled")
            steps = psem("front_steps")
            blank = psem("windows_blank")
            block = phase.enter_context(nc.Block())

            def fours(engine, body):
                for s in range(4):
                    body(s, s, 0)
                with engine.Fori(1, 12) as i:
                    for u in range(4):
                        body(4 * i + u, u, i)
                for s in range(48, GROUPS):
                    body(s, s % 4, s // 4)

            def more(s, ahead=1):
                return not isinstance(s, int) or s + ahead < GROUPS

            def own_columns(t):
                return AGG[t % 4][:, 0:3 * P].rearrange("p (a t w) -> p a t w", a=3, t=QUAD)[:, :, t % QUAD, :]

            @block.gpsimd
            def _(pool):
                def group(s, u, i):
                    pool.wait_ge(idx_ready, s + 1)
                    wait(pool, agg_ready, GROUP * (s - 3))
                    pool.sem_inc(gate, 1)
                    for t in range(GROUP):
                        nc.gpsimd.indirect_dma_start(
                            out=rows[:, u, t, :], out_offset=None, in_=xp_dram[:, :],
                            in_offset=bass.IndirectOffsetOnAxis(ap=idx[:, u, t:t + 1], axis=0),
                        ).then_inc(gathered[u], 16)
                fours(pool, group)

            @block.sync
            def _(sp):
                def fetch(q, p):
                    bases = tile_bases(nc, base_row, ENGINE.SP, GROUP * q)
                    if isinstance(q, int) and q == 0:
                        sp.wait_ge(blank, 1)
                    wait(sp, below_ready, q - 1)
                    for t in range(GROUP):
                        j = t % QUAD
                        sp.dma_start(windows[WINDOW * j:WINDOW * (j + 1), p, t // QUAD, HEADS * j:HEADS * (j + 1)],
                                     adst_dram[bass.ds(bases[t], WINDOW), :]).then_inc(fetched[p], 16)
                    sp.dma_start(cuts[:, p, :], bass.AP(tensor=cut_dram, offset=q * (GROUP * P),
                                                        ap=[[P, GROUP], [0, HEADS], [1, P + 1]])).then_inc(fetched[p], 16)

                def group(s, u, i):
                    if more(s, 2):
                        fetch(s + 2, u % 2)
                fetch(0, 0)
                fetch(1, 1)
                fours(sp, group)

            FETCHES = 16 * (GROUP + 1)

            def fetches(u, i, ahead):
                return FETCHES * (2 * i + (u + ahead) // 2 + 1)

            @block.tensor
            def _(pe):
                def front(q, p, k, fetch_count):
                    if k == 2:
                        pe.wait_ge(hot_ready, q + 1)
                        for g in range(4):
                            last = nc.tensor.transpose(TR[:, P * g:P * (g + 1)], hot[:, p, QUAD * g:QUAD * (g + 1), :].rearrange("p t w -> p (t w)"), ident[:, :])
                        last.then_inc(tr_ready, 1)
                    if k == 4:
                        pe.wait_ge(tr_copied, q + 1)
                        pe.wait_ge(fetched[p], fetch_count)
                        for g in range(4):
                            last = nc.tensor.matmul(LOOK[:, QUAD * HEADS * g:QUAD * HEADS * (g + 1)], hotT[:, P * g:P * (g + 1)],
                                                    windows[:, p, g, :], start=True, stop=True)
                        last.then_inc(looked_up, 1)
                    if k == 7:
                        pe.wait_ge(logits_ready, q + 1)
                        wait(pe, drop_ready, q)
                        nc.tensor.transpose(CHAIN[:, P:2 * P], logits[:, :], ident[:, :]).then_inc(vt_ready, 1)
                    if k == 10:
                        pe.wait_ge(ends_ready, q + 1)
                        pe.wait_ge(below_ready, q + 1)
                        nc.tensor.matmul(CHAIN[0:HEADS, 0:4 * GROUP], head_of[:, :], ends[:, :], start=True, stop=True).then_inc(ends_turned, 1)
                    if k == 11:
                        pe.wait_ge(powers_ready, q + 1)
                        wait(pe, factors_ready, q)
                        nc.tensor.transpose(TURN[:, 0:P], powers[:, :], ident[:, :]).then_inc(weight_turned, 1)
                    if k == 15:
                        pe.wait_ge(drop_exp_ready, q + 1)
                        pe.wait_ge(weight_ready, q + 1)
                        for n in range(3):
                            last = nc.tensor.matmul(TURN[:, P + 32 * n:P + 32 * (n + 1)], spread[0:HEADS, n, :], drop_exp[:, :],
                                                    start=True, stop=True)
                        last.then_inc(factors_spread, 1)

                def group(s, u, i):
                    p = u % 2
                    for t in range(GROUP):
                        if more(s):
                            front(s + 1, 1 - p, t, fetches(u, i, 1))
                        if t % 2 == 0:
                            pe.wait_ge(weighted, 8 * s + t // 2 + 1)
                        wait(pe, agg_free, GROUP * s + t - 3)
                        bank = AGG[t % 4]
                        quad = hot[:, p, QUAD * (t // QUAD):QUAD * (t // QUAD + 1), :].rearrange("p t w -> p (t w)")
                        for k in range(2):
                            nc.tensor.matmul(bank[:, P * k:P * (k + 1)], rows[:, u, t, P * k:P * (k + 1)], quad, start=True, stop=True)
                        nc.tensor.matmul(bank[0:HEADS, 2 * P:3 * P], weight[:, p, HEADS * t:HEADS * (t + 1)], quad, start=True, stop=True).then_inc(agg_ready, 1)

                for k in range(GROUP):
                    front(0, 0, k, FETCHES)
                fours(pe, group)

            @block.scalar
            def _(act):
                def front(q, k):
                    if k == 2:
                        act.wait_ge(tr_ready, q + 1)
                        wait(act, looked_up, q)
                        nc.scalar.copy(hotT[:, :], TR[:, :]).then_inc(tr_copied, 1)
                    if k == 10:
                        act.wait_ge(below_ready, q + 1)
                        nc.scalar.activation(powers[:, :], below[:, :], ACT.Exp).then_inc(powers_ready, 1)
                    if k == 14:
                        act.wait_ge(drop_ready, q + 1)
                        nc.scalar.activation(drop_exp[:, :], drop[:, :], ACT.Exp).then_inc(drop_exp_ready, 1)

                def group(s, u, i):
                    bases = tile_bases(nc, base_row, ENGINE.Activation, GROUP * s)
                    for t in range(GROUP):
                        if more(s):
                            front(s + 1, t)
                        act.wait_ge(agg_ready, GROUP * s + t + 1)
                        wait(act, acc_copied, GROUP * s + t)
                        act.sem_inc(gate, 1)
                        nc.scalar.copy(acc[:, :, bass.ds(bases[t] + 1, WINDOW - 1)], own_columns(t)[:, :, 1:WINDOW]).then_inc(acc_copied, 1)

                for k in range(GROUP):
                    front(0, k)
                fours(act, group)

            @block.vector
            def _(dve):
                def weigh(u, p, g):
                    v = rows[:, u, 2 * g:2 * (g + 1), 0:D].rearrange("p t (h c) -> p t h c", c=C)
                    w = weight[:, p, 2 * HEADS * g:2 * HEADS * (g + 1)].rearrange("p (t h) -> p t h", h=HEADS)
                    nc.vector.tensor_tensor(v, v, w.unsqueeze(3).to_broadcast([P, 2, HEADS, C]), ALU.mult).then_inc(weighted, 1)

                def front(q, p, r, k, order, fetch_count, row_count):
                    if k == 0:
                        wait(dve, agg_ready, GROUP * (q - 1))
                        nc.vector.tensor_tensor(hot[:, p, :, :], iota[:, 0:WINDOW].unsqueeze(1).to_broadcast([P, GROUP, WINDOW]),
                                                relT[:, cols(GROUP * q, GROUP)].unsqueeze(2).to_broadcast([P, GROUP, WINDOW]),
                                                ALU.is_equal).then_inc(hot_ready, 1)
                    if k == 3:
                        dve.wait_ge(fetched[p], fetch_count)
                        wait(dve, ends_turned, q)
                        order.did(nc.vector.tensor_reduce(ends_cut[:, :], cuts[:, p, 0:P], AX.X, ALU.add))
                        order.did(nc.vector.tensor_scalar(ends[:, CUT], tile_of[:, :], cuts[:, p, 0:1], None, ALU.mult))
                        order.settle()
                        order.did(nc.vector.tensor_scalar(ends[:, CUT_SUM], tile_of[:, :], ends_cut[:, 0:1], None, ALU.mult))
                    if k == 5:
                        dve.wait_ge(looked_up, q + 1)
                        dve.wait_ge(gathered[r], row_count)
                        order.did(nc.vector.tensor_tensor(scan_a[:, :], LOOK[:, 0:P], a_edge[:, cols(P * q, P)], ALU.add))
                        order.settle()
                        order.did(nc.vector.tensor_tensor(scan_b[:, :].rearrange("p (t h) -> p t h", h=HEADS),
                                                          scan_a[:, :].rearrange("p (t h) -> p t h", h=HEADS),
                                                          rows[:, r, :, D:XROW], ALU.add))
                        order.settle()
                        nc.vector.scalar_tensor_tensor(out=logits[:, :], in0=scan_b[:, :], scalar=0.2, in1=scan_b[:, :],
                                                       op0=ALU.mult, op1=ALU.max).then_inc(logits_ready, 1)
                    if k == 8:
                        dve.wait_ge(vt_ready, q + 1)
                        order.did(nc.vector.tensor_tensor_scan(scan_a[:, :], cuts[:, p, 0:P], CHAIN[:, P:2 * P], -BIG, ALU.add, ALU.max))
                        order.settle()
                        order.did(nc.vector.tensor_tensor_scan(scan_b[:, ::-1], cuts[:, p, P:0:-1], scan_a[:, ::-1], -BIG, ALU.add, ALU.max))
                        order.settle()
                        nc.vector.tensor_scalar(ends[:, END], tile_of[:, :], scan_a[:, P - 1:P], None, ALU.mult)
                        nc.vector.tensor_scalar(ends[:, FIRST], tile_of[:, :], scan_b[:, 0:1], None, ALU.mult).then_inc(ends_ready, 1)
                        dve.wait_ge(ends_ready, q + 1)
                        nc.vector.tensor_tensor(below[:, :], CHAIN[:, P:2 * P], scan_b[:, :], ALU.subtract).then_inc(below_ready, 1)
                    if k == 13:
                        dve.wait_ge(ends_turned, q + 1)
                        order.did(nc.vector.tensor_copy(ends_row[:, :], CHAIN[0:HEADS, 0:4 * GROUP]))
                        order.settle()
                        order.did(nc.vector.tensor_tensor_scan(running[:, 1:GROUP + 1], ends_row[:, CUT_SUM], ends_row[:, END],
                                                               running[:, 0:1], ALU.add, ALU.max))
                        order.settle()
                        order.did(nc.vector.tensor_tensor(carry[:, :], running[:, 0:GROUP], ends_row[:, CUT], ALU.add))
                        order.settle()
                        order.did(nc.vector.tensor_copy(running[:, 0:1], running[:, GROUP:GROUP + 1]))
                        order.did(nc.vector.tensor_tensor(highest[:, :], carry[:, :], ends_row[:, FIRST], ALU.max))
                        order.settle()
                        nc.vector.tensor_tensor(drop[:, 0:GROUP], carry[:, :], highest[:, :], ALU.subtract)
                        nc.vector.tensor_tensor(drop[:, GROUP:2 * GROUP], ends_row[:, FIRST], highest[:, :], ALU.subtract).then_inc(drop_ready, 1)
                    if k == 12:
                        dve.wait_ge(weight_turned, q + 1)
                        nc.vector.tensor_copy(weight[:, p, :], TURN[:, 0:P]).then_inc(weight_ready, 1)
                    if k == 14:
                        dve.wait_ge(weight_ready, q + 1)
                        weigh(r, p, 0)
                    if k == 15:
                        weigh(r, p, 1)

                WEIGHS = (1, 2, 4, 6, 7, 10)

                def finish_factors(s, p):
                    dve.wait_ge(factors_spread, s + 1)
                    nc.vector.tensor_copy(factor[:, p, :, :].rearrange("p a b -> p (a b)"), TURN[:, P:P + 96]).then_inc(factors_ready, 1)

                def column(base):
                    return acc[:, :, bass.ds(base, 1)].rearrange("p a o -> p (a o)")

                def scale_column(count, base, t, p):
                    dve.wait_ge(acc_copied, count + 1)
                    nc.vector.tensor_tensor(fresh[:, t % 2, :], own_columns(t)[:, :, 0], factor[:, p, :, GROUP + t], ALU.mult)
                    wait(dve, agg_free, count)
                    col = column(base)
                    nc.vector.tensor_tensor(col, col, factor[:, p, :, t], ALU.mult).then_inc(scaled, 1)

                def add_column(count, base, t):
                    dve.wait_ge(scaled, count + 1)
                    col = column(base)
                    nc.vector.tensor_tensor(col, col, fresh[:, t % 2, :], ALU.add).then_inc(agg_free, 1)

                def group(s, u, i):
                    p = u % 2
                    lead = 0 if isinstance(s, int) and s == 0 else LAG
                    bases = tile_bases(nc, base_row, ENGINE.DVE, GROUP * s - lead)
                    order = Order(dve, steps, NSTEP * (s + 1) + 1)
                    for k in range(GROUP):
                        t, half = (k - LAG, p) if k >= LAG else (GROUP + k - LAG, 1 - p)
                        due = k >= LAG or lead
                        if k == LAG:
                            dve.wait_ge(factors_ready, s + 1)
                        if due:
                            scale_column(GROUP * s + k - LAG, bases[k - LAG + lead], t, half)
                        if k == 1:
                            finish_factors(s, p)
                        if k in WEIGHS:
                            weigh(u, p, 2 + WEIGHS.index(k))
                        if more(s):
                            front(s + 1, 1 - p, (u + 1) % 4, k, order, fetches(u, i, 1), 16 * GROUP * (i + (u + 1) // 4 + 1))
                        if k == 12 and more(s, 4):
                            nc.vector.tensor_copy(idx[:, u, :], srcT[:, cols(GROUP * s + 4 * GROUP, GROUP)]).then_inc(idx_ready, 1)
                        if due:
                            add_column(GROUP * s + k - LAG, bases[k - LAG + lead], t)
                    if more(s):
                        assert order.steps == NSTEP, order.steps

                nc.vector.memset(windows[:, :, :, :], 0.0).then_inc(blank, 1)
                for bank in AGG:
                    nc.vector.memset(bank[:, 0:3 * P], 0.0)
                nc.vector.memset(running[:, 0:1], -BIG).then_inc(steps, 1)
                dve.wait_ge(steps, 1)
                for r in range(4):
                    nc.vector.tensor_copy(idx[:, r, :], srcT[:, GROUP * r:GROUP * (r + 1)]).then_inc(idx_ready, 1)
                order = Order(dve, steps, 1)
                for k in range(GROUP):
                    front(0, 0, 0, k, order, FETCHES, 16 * GROUP)
                assert order.steps == NSTEP, order.steps
                fours(dve, group)
                bases = tile_bases(nc, base_row, ENGINE.DVE, TILES - GROUP)
                for t in range(GROUP - LAG, GROUP):
                    scale_column(TILES - GROUP + t, bases[t], t, (GROUPS - 1) % 2)
                    add_column(TILES - GROUP + t, bases[t], t)

        taken[0] = 0
        with ExitStack() as phase:
            g = General(phase, "general1", carve)
            at_dst, mixed, best, m_new, m_old = (carve(HEADS) for _ in range(5))
            found = carve(HEADS + 1)
            diagonal = carve(HEADS + 1, P)
            masked = carve(HEADS, P)
            unlike = carve(P)
            lowest = carve(ACC // P * HEADS)
            exps = carve(HEADS)

            def psem(name):
                return phase.enter_context(nc.semaphore(name))
            logits_made, rows_spread = psem("general1_logits_made"), psem("general1_rows_spread")
            table_blank, table_stored = psem("general1_lowest_made"), psem("general1_table_stored")
            maxima_loaded, maxima_made, maxima_stored = psem("general1_maxima_loaded"), psem("general1_maxima_made"), psem("general1_maxima_stored")
            below_made, exps_made, weighed = psem("general1_below_made"), psem("general1_exps_made"), psem("general1_weighed")
            steps = psem("general1_vector_steps")
            block = phase.enter_context(nc.Block())

            @block.gpsimd
            def _(pool):
                with pool.If(is_general(pool) != 0):
                    g.load_bases(pool)
                    g.number_nodes()
                    pool.wait_ge(table_blank, 1)
                    pool.dma_start(max_dram[:, :].rearrange("(p k) h -> p (k h)", p=P), lowest).then_inc(table_stored, 16)
                    pool.wait_ge(table_stored, 16)
                    with pool.Fori(0, TILES) as t:
                        pool.wait_ge(g.indexed, t + 1)
                        g.gather(pool, g.row, xp_dram[:, :], 0, g.loaded)
                        g.gather(pool, at_dst, adst_dram[:, :], 1, g.loaded)
                        g.gather(pool, m_old, max_dram[:, :], 1, maxima_loaded)
                        pool.wait_ge(maxima_made, t + 1)
                        pool.sem_inc(gate, 1)
                        nc.gpsimd.indirect_dma_start(
                            out=max_dram[:, :], out_offset=bass.IndirectOffsetOnAxis(ap=idx[:, 0, 1:2], axis=0),
                            in_=m_new, in_offset=None).then_inc(maxima_stored, 16)
                        pool.wait_ge(maxima_stored, 16 * t + 16)
                    with pool.Fori(0, TILES) as t:
                        pool.wait_ge(g.indexed, t + (TILES + 1))
                        g.gather(pool, g.row, xp_dram[:, :], 0, g.loaded)
                        g.gather(pool, m_old, max_dram[:, :], 1, maxima_loaded)

            @block.tensor
            def _(pe):
                with pe.If(is_general(pe) != 0):
                    g.spread_bases(pe)
                    with pe.Fori(0, TILES) as t:
                        pe.wait_ge(logits_made, t + 1)
                        for n in range(2):
                            nc.tensor.matmul(PS[n][:, :], g.unit, diagonal[:, 4 * n:4 * n + 4, :].rearrange("p h e -> p (h e)"),
                                             start=True, stop=True)
                        nc.tensor.matmul(PS[2][:, 0:P], g.unit, diagonal[:, HEADS, :], start=True, stop=True).then_inc(rows_spread, 1)
                    with pe.Fori(0, TILES) as t:
                        pe.wait_ge(weighed, t + 1)
                        g.sum_tile(pe, t, exps)

            @block.scalar
            def _(act):
                with act.If(is_general(act) != 0):
                    with act.Fori(0, TILES) as t:
                        act.wait_ge(below_made, t + 1)
                        nc.scalar.activation(exps, mixed, ACT.Exp).then_inc(exps_made, 1)

            @block.vector
            def _(dve):
                with dve.If(is_general(dve) != 0):
                    nc.vector.memset(lowest, -BIG).then_inc(table_blank, 1)
                    g.prepare(dve)
                    with dve.Fori(0, TILES) as t:
                        order = Order(dve, steps, 7 * t)
                        g.index_tile(dve, t)
                        dve.wait_ge(g.loaded, 32 * t + 32)
                        mine = a_edge[:, cols(HEADS * t, HEADS)]
                        order.did(nc.vector.tensor_tensor(mixed, at_dst, mine, ALU.add))
                        order.settle()
                        order.did(nc.vector.tensor_tensor(mixed, mixed, g.row[:, D:XROW], ALU.add))
                        order.settle()
                        order.did(nc.vector.scalar_tensor_tensor(out=found[:, 0:HEADS], in0=mixed, scalar=0.2, in1=mixed,
                                                                 op0=ALU.mult, op1=ALU.max))
                        order.did(nc.vector.tensor_copy(found[:, HEADS:HEADS + 1], g.dst_of[:, cols(t, 1)]))
                        order.settle()
                        dve.sem_inc(gate, 1)
                        nc.vector.tensor_copy(mine, found[:, 0:HEADS])
                        nc.vector.tensor_tensor(diagonal, ident[:, :].unsqueeze(1).to_broadcast([P, HEADS + 1, P]),
                                                found.unsqueeze(2).to_broadcast([P, HEADS + 1, P]), ALU.mult).then_inc(logits_made, 1)
                        dve.wait_ge(rows_spread, t + 1)
                        order.did(nc.vector.tensor_scalar(unlike, PS[2][:, 0:P], found[:, HEADS:HEADS + 1], -BIG, ALU.not_equal, ALU.mult))
                        order.settle()
                        for n in range(2):
                            last = nc.vector.tensor_tensor(masked[:, 4 * n:4 * n + 4, :], PS[n][:, :].rearrange("p (h e) -> p h e", h=4),
                                                           unlike.unsqueeze(1).to_broadcast([P, 4, P]), ALU.add)
                        order.did(last)
                        order.settle()
                        order.did(nc.vector.tensor_reduce(best, masked, AX.X, ALU.max))
                        order.settle()
                        dve.wait_ge(maxima_loaded, 16 * t + 16)
                        nc.vector.tensor_tensor(m_new, best, m_old, ALU.max).then_inc(maxima_made, 1)
                        dve.wait_ge(maxima_stored, 16 * t + 16)
                        assert order.steps == 7
                    with dve.Fori(0, TILES) as t:
                        g.index_tile(dve, t)
                        dve.wait_ge(maxima_loaded, 16 * t + 16 * (TILES + 1))
                        nc.vector.tensor_tensor(mixed, a_edge[:, cols(HEADS * t, HEADS)], m_old, ALU.subtract).then_inc(below_made, 1)
                        g.mark_nodes(dve, t)
                        dve.wait_ge(exps_made, t + 1)
                        dve.wait_ge(g.loaded, 16 * t + (32 * TILES + 16))
                        heads = g.row[:, 0:D].rearrange("p (h c) -> p h c", c=C)
                        nc.vector.tensor_tensor(heads, heads, exps.unsqueeze(2).to_broadcast([P, HEADS, C]), ALU.mult).then_inc(weighed, 1)
                        g.add_tile(dve, t)

        taken[0] = 0
        x1_in = carve(UNROLL, D)
        staged3 = carve(RING, 3 * P)
        x1_bias, x1_beta, y1, t1, g1, y2, result = (carve(RING, D) for _ in range(7))
        bias_all, gamma_all, beta_all = carve(D), carve(D), carve(D)
        stats, moments, spreads = carve(RING, 6), carve(RING, 2), carve(RING, 4)
        stats2, moments2, spreads2 = carve(RING, 6), carve(RING, 2), carve(RING, 4)
        rden = carve(RING, HEADS)

        with ExitStack() as phase:
            def psem(name):
                return phase.enter_context(nc.semaphore(name))
            vectors = psem("vectors_loaded")
            x1_loaded = [psem(f"x1_loaded{p}") for p in range(RING)]
            staged_ready, sums_turned = psem("sums_staged"), psem("sums_turned")
            bias_added, beta_added = psem("bias_added"), psem("beta_added")
            y1_made, var1_ready, sd1_ready = psem("y1_made"), psem("var1_ready"), psem("sd1_ready")
            t1_made, g1_made = psem("t1_made"), psem("g1_made")
            y2_made, var2_ready, sd2_ready, result_made = psem("y2_made"), psem("var2_ready"), psem("sd2_ready"), psem("result_made")
            stored = [psem(f"stored{p}") for p in range(RING)]
            y1_added = psem("y1_added")
            add_steps, add2_steps = psem("add_steps"), psem("add2_steps")
            norm_steps, norm2_steps = psem("norm_steps"), psem("norm2_steps")
            TURN_SUMS, ADD, ROOT, NORM, SCALE, ADD2, ROOT2, NORM2, STORE = 1, 2, 2, 3, 3, 4, 4, 5, 5
            block = phase.enter_context(nc.Block())

            @block.sync
            def _(sp):
                for v, a in ((bias_all, bias), (gamma_all, gamma), (beta_all, beta)):
                    sp.dma_start(v, a.partition_broadcast(P)).then_inc(vectors, 16)

                def slot(j, u, turn):
                    if inside(j):
                        wait(sp, bias_added, j - RING + 1)
                        sp.sem_inc(gate, 1)
                        wait(sp, beta_added, j - UNROLL + 1)
                        sp.dma_start(x1_in[:, u, :], x1_dram[cols(j * P, P), :]).then_inc(x1_loaded[u % RING], 16)
                    if inside(j - STORE):
                        b, r = j - STORE, (u - STORE) % RING
                        sp.wait_ge(result_made, b + 1)
                        n = last_rows if isinstance(b, int) and b == BLOCKS - 1 else P
                        sp.dma_start(out[cols(b * P, n), :], result[0:n, r, :]).then_inc(stored[r], 16)
                staggered(sp, slot, STORE)
                for r in range(RING):
                    sp.wait_ge(stored[r], 16 * uses(r, RING))

            @block.gpsimd
            def _(pool):
                pool.wait_ge(vectors, 48)

                def slot(j, u, turn):
                    if inside(j - TURN_SUMS):
                        b, v = j - TURN_SUMS, (u - TURN_SUMS) % UNROLL
                        pool.wait_ge(x1_loaded[v % RING], 16 * turn(TURN_SUMS, RING) + 16)
                        wait(pool, y1_added, b - RING + 1)
                        nc.gpsimd.tensor_tensor(x1_bias[:, v % RING, :], x1_in[:, v, :], bias_all, ALU.add).then_inc(bias_added, 1)
                    if inside(j - SCALE):
                        b, v, r = j - SCALE, (u - SCALE) % UNROLL, (u - SCALE) % RING
                        wait(pool, y2_made, b - RING + 1)
                        nc.gpsimd.tensor_tensor(x1_beta[:, r, :], x1_in[:, v, :], beta_all, ALU.add).then_inc(beta_added, 1)
                        pool.wait_ge(t1_made, b + 1)
                        nc.gpsimd.tensor_tensor(g1[:, r, :], t1[:, r, :], gamma_all, ALU.mult).then_inc(g1_made, 1)
                staggered(pool, slot, STORE)

            @block.tensor
            def _(pe):
                def slot(j, u, turn):
                    if inside(j - TURN_SUMS):
                        b, v = j - TURN_SUMS, u - TURN_SUMS
                        pe.wait_ge(staged_ready, b + 1)
                        wait(pe, y1_made, b - RING + 1)
                        for k in range(3):
                            last = nc.tensor.transpose(PS[v % RING][:, P * k:P * (k + 1)], staged3[:, v % RING, P * k:P * (k + 1)], ident[:, :])
                        last.then_inc(sums_turned, 1)
                staggered(pe, slot, STORE)

            @block.scalar
            def _(act):
                def slot(j, u, turn):
                    if inside(j):
                        wait(act, sums_turned, j - RING + 1)
                        act.sem_inc(gate, 1)
                        nc.scalar.copy(staged3[:, u % RING, :].rearrange("p (k n) -> p k n", k=3),
                                       acc[:, :, cols(j * P, P)]).then_inc(staged_ready, 1)
                    if inside(j - NORM):
                        b, r = j - NORM, (u - NORM) % RING
                        act.wait_ge(norm_steps, 2 * b + 2)
                        wait(act, g1_made, b - RING + 1)
                        nc.scalar.activation(t1[:, r, :], y1[:, r, :], ACT.Identity, bias=spreads[:, r, 3:4],
                                             scale=spreads[:, r, 2:3]).then_inc(t1_made, 1)
                    if inside(j - ROOT2):
                        b, r = j - ROOT2, (u - ROOT2) % RING
                        act.wait_ge(var2_ready, b + 1)
                        nc.scalar.activation(spreads2[:, r, 1:2], spreads2[:, r, 0:1], ACT.Sqrt).then_inc(sd2_ready, 1)
                    if inside(j - NORM2):
                        b, r = j - NORM2, (u - NORM2) % RING
                        act.wait_ge(norm2_steps, 2 * b + 2)
                        wait(act, stored[r], 16 * turn(NORM2, RING))
                        nc.scalar.activation(result[:, r, :], y2[:, r, :], ACT.Identity, bias=spreads2[:, r, 3:4],
                                             scale=spreads2[:, r, 2:3]).then_inc(result_made, 1)
                    if inside(j - ROOT):
                        b, r = j - ROOT, (u - ROOT) % RING
                        act.wait_ge(var1_ready, b + 1)
                        nc.scalar.activation(spreads[:, r, 1:2], spreads[:, r, 0:1], ACT.Sqrt).then_inc(sd1_ready, 1)
                staggered(act, slot, STORE)

            @block.vector
            def _(dve):
                def slot(j, u, turn):
                    if inside(j - ADD):
                        b, r = j - ADD, (u - ADD) % RING
                        dve.wait_ge(sums_turned, b + 1)
                        nc.vector.tensor_scalar(rden[:, r, :], PS[r][:, 2 * P:2 * P + HEADS], 1.0e-16, None, ALU.add).then_inc(add_steps, 1)
                    if inside(j - ADD2):
                        b, r = j - ADD2, (u - ADD2) % RING
                        dve.wait_ge(g1_made, b + 1)
                        wait(dve, result_made, b - RING + 1)
                        nc.vector.tensor_tensor(y2[:, r, :], g1[:, r, :], x1_beta[:, r, :], ALU.add).then_inc(y2_made, 1)
                    if inside(j - ADD):
                        b, r = j - ADD, (u - ADD) % RING
                        dve.wait_ge(add_steps, 4 * b + 1)
                        nc.vector.reciprocal(rden[:, r, :], rden[:, r, :]).then_inc(add_steps, 1)
                    if inside(j - ADD2):
                        b, r = j - ADD2, (u - ADD2) % RING
                        dve.wait_ge(y2_made, b + 1)
                        nc.vector.bn_stats(stats2[:, r, :], y2[:, r, :]).then_inc(add2_steps, 1)
                    if inside(j - NORM):
                        b, r = j - NORM, (u - NORM) % RING
                        dve.wait_ge(sd1_ready, b + 1)
                        nc.vector.reciprocal(spreads[:, r, 2:3], spreads[:, r, 1:2]).then_inc(norm_steps, 1)
                    if inside(j - NORM2):
                        b, r = j - NORM2, (u - NORM2) % RING
                        dve.wait_ge(sd2_ready, b + 1)
                        nc.vector.reciprocal(spreads2[:, r, 2:3], spreads2[:, r, 1:2]).then_inc(norm2_steps, 1)
                    if inside(j - ADD):
                        b, r = j - ADD, (u - ADD) % RING
                        dve.wait_ge(add_steps, 4 * b + 2)
                        wait(dve, t1_made, b - RING + 1)
                        nc.vector.tensor_tensor(y1[:, r, :].rearrange("p (h c) -> p h c", c=C),
                                                PS[r][:, 0:D].rearrange("p (h c) -> p h c", c=C),
                                                rden[:, r, :].unsqueeze(2).to_broadcast([P, HEADS, C]), ALU.mult).then_inc(y1_made, 1)
                    if inside(j - NORM):
                        b, r = j - NORM, (u - NORM) % RING
                        dve.wait_ge(norm_steps, 2 * b + 1)
                        nc.vector.scalar_tensor_tensor(out=spreads[:, r, 3:4], in0=moments[:, r, 0:1], scalar=-1.0, in1=spreads[:, r, 2:3],
                                                       op0=ALU.mult, op1=ALU.mult).then_inc(norm_steps, 1)
                    if inside(j - ADD2):
                        b, r = j - ADD2, (u - ADD2) % RING
                        dve.wait_ge(add2_steps, 2 * b + 1)
                        dve.sem_inc(gate, 1)
                        nc.vector.bn_aggr(moments2[:, r, :], stats2[:, r, :]).then_inc(add2_steps, 1)
                    if inside(j - ADD):
                        b, r = j - ADD, (u - ADD) % RING
                        dve.wait_ge(y1_made, b + 1)
                        dve.wait_ge(bias_added, b + 1)
                        nc.vector.tensor_tensor(y1[:, r, :], y1[:, r, :], x1_bias[:, r, :], ALU.add).then_inc(y1_added, 1)
                    if inside(j - NORM2):
                        b, r = j - NORM2, (u - NORM2) % RING
                        dve.wait_ge(norm2_steps, 2 * b + 1)
                        nc.vector.scalar_tensor_tensor(out=spreads2[:, r, 3:4], in0=moments2[:, r, 0:1], scalar=-1.0, in1=spreads2[:, r, 2:3],
                                                       op0=ALU.mult, op1=ALU.mult).then_inc(norm2_steps, 1)
                    if inside(j - ADD2):
                        b, r = j - ADD2, (u - ADD2) % RING
                        dve.wait_ge(add2_steps, 2 * b + 2)
                        nc.vector.tensor_scalar(spreads2[:, r, 0:1], moments2[:, r, 1:2], LN_EPS, None, ALU.add).then_inc(var2_ready, 1)
                    if inside(j - ADD):
                        b, r = j - ADD, (u - ADD) % RING
                        dve.wait_ge(y1_added, b + 1)
                        nc.vector.bn_stats(stats[:, r, :], y1[:, r, :]).then_inc(add_steps, 1)
                    if inside(j - ADD):
                        b, r = j - ADD, (u - ADD) % RING
                        dve.wait_ge(add_steps, 4 * b + 3)
                        dve.sem_inc(gate, 1)
                        nc.vector.bn_aggr(moments[:, r, :], stats[:, r, :]).then_inc(add_steps, 1)
                        dve.wait_ge(add_steps, 4 * b + 4)
                        nc.vector.tensor_scalar(spreads[:, r, 0:1], moments[:, r, 1:2], LN_EPS, None, ALU.add).then_inc(var1_ready, 1)
                staggered(dve, slot, STORE)


_INS = ['x', 'src', 'dst', 'edge_attr_64', 'L0_gnn_W', 'L0_gnn_b', 'L1_gnn_W', 'L1_gnn_W_e', 'L1_gnn_att_src', 'L1_gnn_att_dst',
        'L1_gnn_att_edge', 'L1_gnn_bias', 'L1_gnn_gamma', 'L1_gnn_beta']


def kernel(**inputs):
    import numpy as _np
    import concourse.bacc as _bacc
    from concourse import mybir as _mybir
    from concourse.bass_utils import run_bass_kernel_spmd as _run

    nc = _bacc.Bacc("TRN2", target_bir_lowering=False, num_devices=1)
    arrays, args = {}, []
    for name in _INS:
        a = _np.ascontiguousarray(inputs[name])
        arrays[f"in_{name}"] = a
        args.append(nc.dram_tensor(f"in_{name}", a.shape, _mybir.dt.from_np(a.dtype), kind="ExternalInput").ap())
    args.append(nc.dram_tensor("out_0", (N, D), _mybir.dt.float32, kind="ExternalOutput").ap())
    gnn_kernel(nc, *args)
    r = _run(nc, [arrays], core_ids=[0])
    return r.results[0]["out_0"]
```
